# Optimizing a Trainium2 kernel written in Bass

```python
import numpy as np
import jax
import jax.numpy as jnp

def _softmax(x, axis=-1):
    return jax.nn.softmax(x, axis=axis)

def _gelu(x):
    return jax.nn.gelu(x, approximate=True)

def _silu(x):
    return jax.nn.silu(x)

def _sigmoid(x):
    return jax.nn.sigmoid(x)

def _layernorm(x, axis=-1, eps=1e-05):
    m = jnp.mean(x, axis=axis, keepdims=True)
    v = jnp.var(x, axis=axis, keepdims=True)
    return (x - m) / jnp.sqrt(v + eps)

def _scatter_add(tgt, idx, src, axis=0):
    return tgt.at[idx].add(src)

def _segment_sum(src, seg, n):
    return jax.ops.segment_sum(src, seg, n)
kernel_name = 'mk_vit_tower_cls_d1_tok_img768_r4_edfae6'

def setup_inputs(seed: int=0):
    np.random.seed(seed)
    _w = jnp.asarray

    def _rec_inputs():
        import jax
        import jax.numpy as jnp
        _rk = jax.random.key(seed)
        x = -0.000348323 + 0.999952 * jax.random.normal(jax.random.fold_in(_rk, 1), (16, 96, 96, 3), jnp.float32)
        cls_tok = 0.02 * jax.random.normal(jax.random.fold_in(_rk, 5), (1, 1, 192), jnp.float32)
        return (x, cls_tok)
    x, cls_tok = _rec_inputs()

    def _L0_tok_setup():
        import jax, jax.numpy as jnp
        import numpy as np
        IMG = 96
        PATCH = 16
        CH = 3
        PROJ = 192
        NP_ = (IMG // PATCH) ** 2
        PDIM = PATCH * PATCH * CH

        def _extract_patches(X):
            B = X.shape[0]
            gh = IMG // PATCH
            x = X.reshape(B, gh, PATCH, gh, PATCH, CH)
            x = x.transpose(0, 1, 3, 2, 4, 5)
            return x.reshape(B, NP_, PDIM)
        key = jax.random.key(seed)
        k1, k2, k3, k4 = jax.random.split(key, 4)
        X = jax.random.normal(k1, (32, IMG, IMG, CH), dtype=jnp.float32)
        W = jax.random.normal(k2, (PDIM, PROJ), dtype=jnp.float32) * (1.0 / np.sqrt(PDIM))
        b = jnp.zeros((PROJ,), dtype=jnp.float32)
        pos_emb = jax.random.normal(k3, (NP_, PROJ), dtype=jnp.float32) * 0.02
        return {'X': X, 'W': W, 'b': b, 'pos_emb': pos_emb}
    _L0_tok_all = _L0_tok_setup()
    _L0_tok_in = {k: v for k, v in _L0_tok_all.items() if k in ('W', 'b', 'pos_emb')}
    del _L0_tok_all

    def _L0_attn_setup():
        import jax, jax.numpy as jnp
        import numpy as np
        N_STATE = 192
        N_HEAD = 12
        D_HEAD = N_STATE // N_HEAD
        M_SLOTS = 100

        def _split_heads(t):
            B, T, _ = t.shape
            return t.reshape(B, T, N_HEAD, D_HEAD).transpose(0, 2, 1, 3)

        def _merge_heads(t):
            B, H, T, D = t.shape
            return t.transpose(0, 2, 1, 3).reshape(B, T, H * D)

        def _attn(q, k, v):
            w = jax.nn.softmax(jnp.einsum('bhqd,bhkd->bhqk', q, k), axis=-1)
            return jnp.einsum('bhqk,bhkd->bhqd', w, v)
        key = jax.random.key(seed)
        ks = jax.random.split(key, 10)
        B, S = (2, 512)
        sc = 0.02
        return {'x': jax.random.normal(ks[0], (B, S, N_STATE), dtype=jnp.float32), 'w_attn': jax.random.normal(ks[1], (N_STATE, 3 * N_STATE), dtype=jnp.float32) * sc, 'b_attn': jnp.zeros((3 * N_STATE,), dtype=jnp.float32), 'w_proj': jax.random.normal(ks[2], (N_STATE, N_STATE), dtype=jnp.float32) * sc, 'b_proj': jnp.zeros((N_STATE,), dtype=jnp.float32), 'w_mem': jax.random.normal(ks[3], (N_STATE, 2 * N_STATE), dtype=jnp.float32) * sc, 'b_mem': jnp.zeros((2 * N_STATE,), dtype=jnp.float32), 'w_alpha': jax.random.normal(ks[4], (2 * N_STATE, N_STATE), dtype=jnp.float32) * sc, 'b_alpha': jnp.zeros((N_STATE,), dtype=jnp.float32), 'memory_features': jax.random.normal(ks[5], (1, M_SLOTS, N_STATE), dtype=jnp.float32) * sc}
    _L0_attn_all = _L0_attn_setup()
    _L0_attn_in = {k: v for k, v in _L0_attn_all.items() if k in ('w_attn', 'b_attn', 'w_proj', 'b_proj', 'w_mem', 'b_mem', 'w_alpha', 'b_alpha', 'memory_features')}
    del _L0_attn_all

    def _L0_ffn_setup():
        import jax, jax.numpy as jnp
        import numpy as np
        B, N, D, E, F, K = (2, 512, 192, 8, 768, 2)
        V_MAX = 3.0
        FEAT_CLAMP = 10.0

        def bk_green_diag(a):
            aT = jnp.swapaxes(a, 0, 1)

            def step(c, ai):
                d = ai - 1.0 / c
                return (d, d)
            d0 = aT[0]
            _, d_rest = jax.lax.scan(step, d0, aT[1:])
            d = jnp.concatenate([d0[None], d_rest], axis=0)
            eN = aT[-1]
            _, e_rest = jax.lax.scan(step, eN, aT[:-1], reverse=True)
            e = jnp.concatenate([e_rest, eN[None]], axis=0)
            G = 1.0 / (d + e - aT)
            return jnp.swapaxes(G, 0, 1)
        key = jax.random.key(seed)
        ks = jax.random.split(key, 8)
        s = lambda k, shape, sc: jax.random.normal(k, shape, jnp.float32) * sc
        return {'x': s(ks[0], (B, N, D), 1.0), 'v_w': s(ks[1], (D,), 0.02), 'v_b': jnp.zeros((), jnp.float32), 'gate_w': s(ks[2], (D, E), 0.02), 'gate_b': jnp.zeros((E,), jnp.float32), 'w1': s(ks[3], (E, D, F), 0.02), 'b1': jnp.zeros((E, F), jnp.float32), 'w2': s(ks[4], (E, F, D), 0.02), 'b2': jnp.zeros((E, D), jnp.float32), 'out_w': s(ks[5], (2, D), 0.02), 'out_b': jnp.zeros((D,), jnp.float32), 'bk_scale': jnp.ones((D,), jnp.float32)}
    _L0_ffn_all = _L0_ffn_setup()
    _L0_ffn_in = {k: v for k, v in _L0_ffn_all.items() if k in ('v_w', 'v_b', 'gate_w', 'gate_b', 'w1', 'b1', 'w2', 'b2', 'out_w', 'out_b', 'bk_scale')}
    del _L0_ffn_all
    return {'x': x, 'cls_tok': cls_tok, 'L0_tok_W': _L0_tok_in['W'], 'L0_tok_b': _L0_tok_in['b'], 'L0_tok_pos_emb': _L0_tok_in['pos_emb'], 'L0_attn_w_attn': _L0_attn_in['w_attn'], 'L0_attn_b_attn': _L0_attn_in['b_attn'], 'L0_attn_w_proj': _L0_attn_in['w_proj'], 'L0_attn_b_proj': _L0_attn_in['b_proj'], 'L0_attn_w_mem': _L0_attn_in['w_mem'], 'L0_attn_b_mem': _L0_attn_in['b_mem'], 'L0_attn_w_alpha': _L0_attn_in['w_alpha'], 'L0_attn_b_alpha': _L0_attn_in['b_alpha'], 'L0_attn_memory_features': _L0_attn_in['memory_features'], 'L0_ffn_v_w': _L0_ffn_in['v_w'], 'L0_ffn_v_b': _L0_ffn_in['v_b'], 'L0_ffn_gate_w': _L0_ffn_in['gate_w'], 'L0_ffn_gate_b': _L0_ffn_in['gate_b'], 'L0_ffn_w1': _L0_ffn_in['w1'], 'L0_ffn_b1': _L0_ffn_in['b1'], 'L0_ffn_w2': _L0_ffn_in['w2'], 'L0_ffn_b2': _L0_ffn_in['b2'], 'L0_ffn_out_w': _L0_ffn_in['out_w'], 'L0_ffn_out_b': _L0_ffn_in['out_b'], 'L0_ffn_bk_scale': _L0_ffn_in['bk_scale']}

def reference(x, cls_tok, L0_tok_W, L0_tok_b, L0_tok_pos_emb, L0_attn_w_attn, L0_attn_b_attn, L0_attn_w_proj, L0_attn_b_proj, L0_attn_w_mem, L0_attn_b_mem, L0_attn_w_alpha, L0_attn_b_alpha, L0_attn_memory_features, L0_ffn_v_w, L0_ffn_v_b, L0_ffn_gate_w, L0_ffn_gate_b, L0_ffn_w1, L0_ffn_b1, L0_ffn_w2, L0_ffn_b2, L0_ffn_out_w, L0_ffn_out_b, L0_ffn_bk_scale):
    import jax
    import jax.numpy as jnp

    def _L0_tok_ref(X, W, b, pos_emb):
        import jax, jax.numpy as jnp
        import numpy as np
        IMG = 96
        PATCH = 16
        CH = 3
        PROJ = 192
        NP_ = (IMG // PATCH) ** 2
        PDIM = PATCH * PATCH * CH

        def _extract_patches(X):
            B = X.shape[0]
            gh = IMG // PATCH
            x = X.reshape(B, gh, PATCH, gh, PATCH, CH)
            x = x.transpose(0, 1, 3, 2, 4, 5)
            return x.reshape(B, NP_, PDIM)
        p = _extract_patches(X)
        proj = jnp.einsum('bnd,de->bne', p, W) + b
        return proj + pos_emb[None, :, :]

    def _L0_attn_ref(x, w_attn, b_attn, w_proj, b_proj, w_mem, b_mem, w_alpha, b_alpha, memory_features):
        import jax, jax.numpy as jnp
        import numpy as np
        N_STATE = 192
        N_HEAD = 12
        D_HEAD = N_STATE // N_HEAD
        M_SLOTS = 100

        def _split_heads(t):
            B, T, _ = t.shape
            return t.reshape(B, T, N_HEAD, D_HEAD).transpose(0, 2, 1, 3)

        def _merge_heads(t):
            B, H, T, D = t.shape
            return t.transpose(0, 2, 1, 3).reshape(B, T, H * D)

        def _attn(q, k, v):
            w = jax.nn.softmax(jnp.einsum('bhqd,bhkd->bhqk', q, k), axis=-1)
            return jnp.einsum('bhqk,bhkd->bhqd', w, v)
        B, S, _ = x.shape
        qkv = x @ w_attn + b_attn
        q, k, v = jnp.split(qkv, 3, axis=-1)
        q = _split_heads(q)
        k = _split_heads(k)
        v = _split_heads(v)
        a = _merge_heads(_attn(q, k, v))
        mem = jnp.broadcast_to(memory_features, (B, M_SLOTS, N_STATE))
        mkv = mem @ w_mem + b_mem
        mk, mv = jnp.split(mkv, 2, axis=-1)
        mk = _split_heads(mk)
        mv = _split_heads(mv)
        a1 = _merge_heads(_attn(q, mk, mv))
        alpha = jax.nn.sigmoid(jnp.concatenate([a, a1], axis=-1) @ w_alpha + b_alpha)
        fused = alpha * a + (1.0 - alpha) * a1
        return fused @ w_proj + b_proj

    def _L0_ffn_ref(x, v_w, v_b, gate_w, gate_b, w1, b1, w2, b2, out_w, out_b, bk_scale):
        import jax, jax.numpy as jnp
        import numpy as np
        B, N, D, E, F, K = (2, 512, 192, 8, 768, 2)
        V_MAX = 3.0
        FEAT_CLAMP = 10.0

        def bk_green_diag(a):
            aT = jnp.swapaxes(a, 0, 1)

            def step(c, ai):
                d = ai - 1.0 / c
                return (d, d)
            d0 = aT[0]
            _, d_rest = jax.lax.scan(step, d0, aT[1:])
            d = jnp.concatenate([d0[None], d_rest], axis=0)
            eN = aT[-1]
            _, e_rest = jax.lax.scan(step, eN, aT[:-1], reverse=True)
            e = jnp.concatenate([e_rest, eN[None]], axis=0)
            G = 1.0 / (d + e - aT)
            return jnp.swapaxes(G, 0, 1)
        v = jnp.clip(x @ v_w + v_b, -V_MAX, V_MAX)
        a = (-2.0 + v).astype(jnp.complex64) - 1j
        G = bk_green_diag(a)
        feats = jnp.stack([G.real, G.imag], axis=-1)
        logits = x @ gate_w + gate_b
        probs = jax.nn.softmax(logits, axis=-1)
        topv, topi = jax.lax.top_k(probs, K)
        topv = topv / jnp.sum(topv, axis=-1, keepdims=True)
        comb = jnp.sum(topv[..., None] * jax.nn.one_hot(topi, E, dtype=x.dtype), axis=2)
        h = jax.nn.gelu(jnp.einsum('bnd,edf->bnef', x, w1) + b1)
        y = jnp.einsum('bnef,efd->bned', h, w2) + b2
        ffn_out = jnp.einsum('bne,bned->bnd', comb, y)
        feats_c = jnp.clip(feats, -FEAT_CLAMP, FEAT_CLAMP)
        spec_out = feats_c @ out_w + out_b
        return ffn_out + bk_scale * spec_out
    h = _L0_tok_ref(x, L0_tok_W, L0_tok_b, L0_tok_pos_emb)
    h = jnp.concatenate([jnp.broadcast_to(cls_tok, (h.shape[0], 1, h.shape[2])), h], axis=1)
    h = h + _L0_attn_ref(_layernorm(h, axis=-1), L0_attn_w_attn, L0_attn_b_attn, L0_attn_w_proj, L0_attn_b_proj, L0_attn_w_mem, L0_attn_b_mem, L0_attn_w_alpha, L0_attn_b_alpha, L0_attn_memory_features)
    h = h + _L0_ffn_ref(_layernorm(h, axis=-1), L0_ffn_v_w, L0_ffn_v_b, L0_ffn_gate_w, L0_ffn_gate_b, L0_ffn_w1, L0_ffn_b1, L0_ffn_w2, L0_ffn_b2, L0_ffn_out_w, L0_ffn_out_b, L0_ffn_bk_scale)
    return h

_drawn_inputs = setup_inputs


def setup_inputs(seed=0):
    import zlib

    import numpy as np

    out = dict(_drawn_inputs(seed))
    spreads = {'L0_tok_b': (0.0, 0.1),
     'L0_attn_b_attn': (0.0, 0.375),
     'L0_attn_b_proj': (0.0, 0.1),
     'L0_attn_b_mem': (0.0, 0.557),
     'L0_attn_b_alpha': (0.0, 0.8),
     'L0_ffn_gate_b': (0.0, 0.1),
     'L0_ffn_b1': (0.0, 0.336),
     'L0_ffn_b2': (0.0, 0.1),
     'L0_ffn_out_b': (0.0, 0.1),
     'L0_ffn_bk_scale': (1.0, 0.6)}
    factors = {'cls_tok': 5.393,
     'L0_attn_w_attn': 5.569,
     'L0_attn_w_mem': 8.0,
     'L0_attn_w_alpha': 8.0,
     'L0_attn_memory_features': 8.0,
     'L0_ffn_v_w': 8.0,
     'L0_ffn_out_w': 4.751}
    for name, (base, spread) in spreads.items():
        noise = np.random.default_rng([zlib.crc32(name.encode()), seed]).standard_normal(out[name].shape)
        drawn = base * np.exp(spread * noise) if base else spread * noise
        out[name] = jnp.asarray(drawn.astype(out[name].dtype))
    for name, factor in factors.items():
        out[name] = (out[name] * factor).astype(out[name].dtype)
    return out
```

```python
from contextlib import ExitStack

import concourse.bass as bass
from concourse import mybir

ALU = mybir.AluOpType
ACT = mybir.ActivationFunctionType
F32 = mybir.dt.float32
U32 = mybir.dt.uint32
AX_X = mybir.AxisListType.X

P = 128


def vit_block(nc, x, cls_tok, tok_w, tok_b, pos_emb, w_attn, b_attn, w_proj, b_proj, w_mem, b_mem, w_alpha, b_alpha,
              memory, v_w, v_b, gate_w, gate_b, w1, b1, w2, b2, out_w, out_b, bk_scale, consts, out):
    B, IMG, _, CH = x.shape
    PDIM, D = tok_w.shape
    GRID = 6
    PATCH = IMG // GRID
    NP_ = GRID * GRID
    S = NP_ + 1
    N = B * S
    N2 = N // 2
    NH, DH = 12, 16
    M = memory.shape[1]
    E, _, F = w1.shape
    DA, DB = P, D - P
    T = -(-N // P)
    ROWS = [min(P, N - P * t) for t in range(T)]
    ROW = CH * PATCH
    IH = 2
    CK = PDIM // P
    GW = GRID
    FM = F // P
    U = B // 2

    with ExitStack() as ctx:
        def sb(name, shape, dt=F32):
            return ctx.enter_context(nc.sbuf_tensor(name, shape, dt))

        def sem(name):
            return ctx.enter_context(nc.semaphore(name))

        ps = ctx.enter_context(nc.psum_tensor("ps", [P, 8, 512], F32))
        psf = ps[:, :, :].rearrange("p a b -> p (a b)")

        cst = sb("cst", [P, 128 + 4 + D + 8 + 2])
        ident = cst[:, 0:128]
        headmask = cst[:, 128:132]
        vmask = cst[0:2 * S, 132:132 + D]
        iota8 = cst[:, 132 + D:140 + D]
        halfmask = cst[:, 140 + D:142 + D]

        early = sb("early", [P, 2 * PATCH * IMG * CH])
        xs = early[0:B * GRID, 0:PATCH * IMG * CH].rearrange("p (i j) -> p i j", i=PATCH)
        xp = early[0:B * GRID, PATCH * IMG * CH:].rearrange("p (g i j) -> p g i j", g=GW, i=PATCH)
        hT = early[:, 0:2 * FM * N].rearrange("p (w f n) -> p w f n", w=2, f=FM)
        wt = sb("wt", [P, CK, D])
        pT = sb("pT", [P, CK, B, S])
        sel = sb("sel", [S, B, S])
        pc = sb("pc", [S, D])
        bb = sb("bb", [S, D])
        h = sb("h", [P, T, D])
        xn = sb("xn", [P, T, D])
        st6 = sb("st6", [P, T, 6])
        mv = sb("mv", [P, T, 2])
        eps = sb("eps", [P, T])
        half = sb("half", [P, T])
        rstd = sb("rstd", [P, T])
        xTa = sb("xTa", [P, N])
        xTb = sb("xTb", [DB + 1, N])
        xra = sb("xra", [P, B, 2, S])
        xrb = sb("xrb", [DB + 1, B, 2, S])
        waa = sb("waa", [P, 3 * D])
        wab = sb("wab", [DB + 1, 3 * D])
        qa = sb("qa", [P, 2, N + 64])
        qb = sb("qb", [DB, N + 64])
        kda = sb("kda", [P, 4, N])
        kdb = sb("kdb", [DB, 4, N])
        mf = sb("mf", [M, D])
        mTa = sb("mTa", [P, M])
        mTb = sb("mTb", [DB + 1, M])
        wma = sb("wma", [P, 2 * D])
        wmb = sb("wmb", [DB + 1, 2 * D])
        mkda = sb("mkda", [P, 4, M])
        mkdb = sb("mkdb", [DB, 4, M])
        mvz = sb("mvz", [M, NH, 32])
        NE_ = 4
        Eb = sb("Eb", [P, NE_, 512])
        mx = sb("mx", [P, NE_, NH])
        sm = sb("sm", [P, NE_, NH])
        rs = sb("rs", [P, NE_, NH])
        NPT = 3
        PTs = sb("PTs", [P, NPT, 512])
        vbd = sb("vbd", [2 * S, 2, 2, D])
        aTa = sb("aTa", [P, N])
        aTb = sb("aTb", [DB, N])
        mTa1 = sb("mTa1", [P, N])
        mTb1 = sb("mTb1", [DB + 1, N])
        wal = sb("wal", [P, 4, D])
        tha = sb("tha", [P, N])
        thb = sb("thb", [DB, N])
        fTa = sb("fTa", [P, N])
        fTb = sb("fTb", [DB + 1, N])
        wpa = sb("wpa", [P, D])
        wpb = sb("wpb", [DB + 1, D])
        gva = sb("gva", [P, E])
        gvb = sb("gvb", [DB + 1, E])
        vwa = sb("vwa", [P, 1])
        vwb = sb("vwb", [DB + 1, 1])
        lg = sb("lg", [P, T, E])
        m8 = sb("m8", [P, T, 8])
        i8 = sb("i8", [P, T, 8], U32)
        i8f = sb("i8f", [P, T, 2])
        g1 = sb("g1", [P, T])
        g2 = sb("g2", [P, T])
        c0 = sb("c0", [P, T])
        c1 = sb("c1", [P, T])
        comb = sb("comb", [P, T, E])
        comb1 = sb("comb1", [P, T, E])
        vrow = sb("vrow", [1, N])
        vrev = sb("vrev", [1, N])
        ar = sb("ar", [2 * B, S])
        asg = sb("asg", [2 * B, S])
        dre = sb("dre", [2 * B, S, 2])
        dsq = sb("dsq", [2 * B, 2])
        dn = sb("dn", [2 * B, 1])
        dri = sb("dri", [2 * B, 1])
        altn = sb("altn", [2 * B, S])
        one32 = sb("one32", [2 * B, 1])
        bw = sb("bw", [B, S, 2])
        z = sb("z", [B, S, 2])
        zz = sb("zz", [B, S, 2])
        zn = sb("zn", [B, S])
        zr = sb("zr", [B, S])
        ft = sb("ft", [B, 2, S])
        feats = sb("feats", [3, N])
        ow = sb("ow", [3, D])
        bk = sb("bk", [3, D])
        b2s = sb("b2s", [E, D])
        ones = sb("ones", [1, P])
        W1A = sb("W1A", [P, 2, F])
        W1B = sb("W1B", [DB + 1, 2, F])
        W2 = sb("W2", [P, 2, FM, D])
        B2 = sb("B2", [1, 2, D])
        acc = sb("acc", [P, T, D])

        s_cst = sem("consts_landed")
        s_x = [sem(f"image_rows_landed{i}") for i in range(IH)]
        s_wt = sem("patch_weights_landed")
        s_pos = sem("positions_landed")
        s_mem = sem("memory_landed")
        s_wat = sem("attn_weights_landed")
        s_wal = sem("alpha_weights_landed")
        s_gw = sem("gate_weights_landed")
        s_ow = sem("spec_weights_landed")
        s_set = sem("pool_setup")
        s_sel = sem("selector_ready")
        s_pc = sem("positions_ready")
        s_mt = sem("memory_transposed")
        s_mtc = sem("memory_transposed_copied")
        s_mkv = sem("memory_kv_ready")
        s_mkc = sem("memory_keys_spread")
        s_mvc = sem("memory_values_spread")
        s_xp = sem("patch_rows_gathered")
        s_xr = sem("tokens_repeated")
        s_pt = sem("patches_transposed")
        s_ptc_a = sem("patches_copied_by_act")
        s_ptc_v = sem("patches_copied_by_dve")
        s_tok = sem("tokens_summed")
        s_h = sem("tokens_copied")
        s_st = sem("moments_taken")
        s_ag = sem("mean_and_variance")
        s_ve = sem("variance_plus_eps")
        s_rstd = sem("rstd_ready")
        s_xn = sem("tokens_normalised")
        s_xt = sem("tokens_transposed")
        s_xtc = sem("tokens_transposed_copied")
        s_q = sem("queries_summed")
        s_qc = sem("queries_copied")
        s_k = sem("keys_summed")
        s_kc_a = sem("keys_spread_by_act")
        s_kc_v = sem("keys_spread_by_dve")
        s_v = sem("values_summed")
        s_vc = sem("values_masked")
        s_sc = sem("scores_ready")
        s_mx = sem("score_maxima")
        s_sub = sem("scores_shifted")
        s_exp = sem("exps_ready")
        s_sum = sem("exp_sums")
        s_ri = sem("sum_reciprocals")
        s_pr = sem("probs_ready")
        s_tp = sem("probs_transposed")
        s_tpc = sem("probs_transposed_copied")
        s_o = sem("heads_summed")
        s_oc = sem("heads_copied")
        s_al = sem("alpha_summed")
        s_th = sem("tanh_ready")
        s_df = sem("differences_ready")
        s_fu = sem("fused_products")
        s_ft = sem("fused_ready")
        s_pj = sem("projection_summed")
        s_gt = sem("gates_summed")
        s_vr = sem("potentials_summed")
        s_vrc = sem("potentials_clipped")
        s_lg = sem("logits_copied")
        s_tk = sem("top2_steps")
        s_g1 = sem("gate_differences")
        s_g2 = sem("gate_exps")
        s_ar = sem("scan_inputs_landed")
        s_sn = sem("scan_steps_pool")
        s_sv = sem("scan_steps_dve")
        s_bwd = sem("backward_landed")
        s_z = sem("green_steps")
        s_fe = sem("features_landed")
        s_owb = sem("spec_weights_scaled")
        s_w = [sem(f"expert_weights_landed{i}") for i in range(2)]
        s_h1 = sem("hidden_summed")
        s_ge = sem("gelu_ready")
        s_y = sem("expert_out_summed")
        s_ac = sem("expert_out_added")
        s_out = sem("out_written")

        block = ctx.enter_context(nc.Block())

        UNITS = []
        for u in range(U):
            UNITS.append(("self", u, 0))
            UNITS += [("mem", *divmod(j, 3)) for j in range(2 * u, min(2 * u + 2, 3 * T))]
        NU = len(UNITS)
        PT0 = []
        k = 0
        for kind, _, _ in UNITS:
            PT0.append(k)
            k += 2 if kind == "self" else 1
        SELF = [i for i in range(NU) if UNITS[i][0] == "self"]
        assert sum(1 for kind, _, _ in UNITS if kind == "mem") == 3 * T
        S_BANK, PT_BANK, O_BANK, V_BANK = [0, 1], [2, 3, 4], [5, 6], 7

        def unit_shape(i):
            kind, a, _ = UNITS[i]
            return (P, NH, S) if kind == "self" else (ROWS[a], 4, M)

        def unit_tile(buf, i):
            m, nh, w = unit_shape(i)
            return buf[0:m, 0:nh * w].rearrange("p (h w) -> p h w", h=nh)

        @block.sync
        def _(sp):
            xv = x.rearrange("b (g i) j c -> (b g) i (j c)", i=PATCH)
            sp.dma_start(cst[:, :], consts).then_inc(s_cst, 16)
            for ih in range(IH):
                sp.dma_start(xs[:, 8 * ih:8 * ih + 8, :], xv[:, 8 * ih:8 * ih + 8, :]).then_inc(s_x[ih], 16)
            sp.dma_start(wt[:, :, :], tok_w.rearrange("(c p) n -> p c n", p=P)).then_inc(s_wt, 16)
            sp.dma_start(waa[:, :], w_attn[0:P, :]).then_inc(s_wat, 16)
            sp.dma_start(wab[0:DB, :], w_attn[P:D, :]).then_inc(s_wat, 16)
            sp.dma_start(wab[DB:DB + 1, :], b_attn.rearrange("(a n) -> a n", a=1)).then_inc(s_wat, 16)
            for j, (r0, r1) in enumerate([(0, 128), (128, 192), (192, 320), (320, 384)]):
                sp.dma_start(wal[0:r1 - r0, j, :], w_alpha[r0:r1, :]).then_inc(s_wal, 16)
            sp.dma_start(wal[DB:DB + 1, 3, :], b_alpha.rearrange("(a n) -> a n", a=1)).then_inc(s_wal, 16)
            sp.dma_start(wpa[:, :], w_proj[0:P, :]).then_inc(s_wal, 16)
            sp.dma_start(wpb[0:DB, :], w_proj[P:D, :]).then_inc(s_wal, 16)
            sp.dma_start(wpb[DB:DB + 1, :], b_proj.rearrange("(a n) -> a n", a=1)).then_inc(s_wal, 16)
            sp.dma_start(gva[:, :], gate_w[0:P, :]).then_inc(s_gw, 16)
            sp.dma_start(gvb[0:DB, :], gate_w[P:D, :]).then_inc(s_gw, 16)
            sp.dma_start(gvb[DB:DB + 1, :], gate_b.rearrange("(a n) -> a n", a=1)).then_inc(s_gw, 16)
            sp.dma_start(vwa[:, :], v_w.rearrange("(p a) -> p a", a=1)[0:P]).then_inc(s_gw, 16)
            sp.dma_start(vwb[0:DB, :], v_w.rearrange("(p a) -> p a", a=1)[P:D]).then_inc(s_gw, 16)
            sp.dma_start(vwb[DB:DB + 1, :], v_b).then_inc(s_gw, 16)
            sp.dma_start(ow[0:2, :], out_w).then_inc(s_ow, 16)
            sp.dma_start(ow[2:3, :], out_b.rearrange("(a n) -> a n", a=1)).then_inc(s_ow, 16)
            for r in range(3):
                sp.dma_start(bk[r:r + 1, :], bk_scale.rearrange("(a n) -> a n", a=1)).then_inc(s_ow, 16)
            for e in range(E):
                w = e % 2
                if e >= 2:
                    sp.wait_ge(s_y, T * (e - 1))
                sp.dma_start(W1A[:, w, :], w1[e, 0:P, :]).then_inc(s_w[w], 16)
                sp.dma_start(W1B[0:DB, w, :], w1[e, P:D, :]).then_inc(s_w[w], 16)
                sp.dma_start(W1B[DB:DB + 1, w, :], b1[e:e + 1, :]).then_inc(s_w[w], 16)
                sp.dma_start(W2[:, w, :, :], w2[e].rearrange("(m p) n -> p m n", p=P)).then_inc(s_w[w], 16)
                sp.dma_start(B2[:, w, :], b2[e:e + 1, :]).then_inc(s_w[w], 16)
            of = out.rearrange("b s d -> (b s) d")
            for t in range(T):
                sp.wait_ge(s_ac, T * E + t + 1)
                sp.dma_start(of[P * t:P * t + ROWS[t], :], acc[0:ROWS[t], t, :]).then_inc(s_out, 16)
            sp.wait_ge(s_out, 16 * T)

        @block.gpsimd
        def _(pool):
            pool.memset(bb[0:1, :], 0.0).then_inc(s_set, 1)
            pool.memset(xTb[:, :], 1.0).then_inc(s_set, 1)
            pool.memset(mTb[:, :], 1.0).then_inc(s_set, 1)
            pool.memset(mvz[:, :, :], 0.0).then_inc(s_set, 1)
            pool.memset(eps[:, :], 1e-5).then_inc(s_set, 1)
            pool.memset(half[:, :], -0.5).then_inc(s_set, 1)
            pool.memset(qa[:, :, N:N + 64], 0.0).then_inc(s_set, 1)
            pool.memset(qb[:, N:N + 64], 0.0).then_inc(s_set, 1)
            pool.memset(mv[:, :, :], 1.0).then_inc(s_set, 1)
            pool.memset(pT[:, :, :, 0:1], 0.0).then_inc(s_set, 1)
            pool.dma_start(mf[:, :], memory[0]).then_inc(s_mem, 16)
            pool.dma_start(wma[:, :], w_mem[0:P, :]).then_inc(s_mem, 16)
            pool.dma_start(wmb[0:DB, :], w_mem[P:D, :]).then_inc(s_mem, 16)
            pool.dma_start(wmb[DB:DB + 1, :], b_mem.rearrange("(a n) -> a n", a=1)).then_inc(s_mem, 16)
            pool.dma_start(pc[0:1, :], cls_tok[0]).then_inc(s_pos, 16)
            pool.dma_start(pc[1:S, :], pos_emb).then_inc(s_pos, 16)
            pool.dma_start(bb[1:S, :], tok_b.rearrange("(a n) -> a n", a=1).broadcast_to([NP_, D])).then_inc(s_pos, 16)
            pool.wait_ge(s_set, 10)
            pool.memset(mTb1[DB:DB + 1, :], 1.0).then_inc(s_set, 1)
            pool.memset(fTb[DB:DB + 1, :], 1.0).then_inc(s_set, 1)
            pool.wait_ge(s_set, 12)
            pool.memset(lg[:, :, :], 0.0).then_inc(s_set, 1)
            pool.memset(m8[:, :, :], 0.0).then_inc(s_set, 1)
            pool.memset(i8[:, :, :], 0).then_inc(s_set, 1)
            pool.memset(one32[:, :], 1.0).then_inc(s_set, 1)
            pool.memset(feats[:, :], 1.0).then_inc(s_set, 1)
            pool.memset(ones[:, :], 1.0).then_inc(s_set, 1)
            pool.memset(altn[:, :], 1.0).then_inc(s_set, 1)
            pool.wait_ge(s_set, 19)
            pool.memset(altn[:, 1:S:2], -1.0).then_inc(s_set, 1)
            pool.wait_ge(s_cst, 16)
            pool.tensor_copy(sel[:, :, :], ident[0:S, None, 0:S].broadcast_to([S, B, S])).then_inc(s_sel, 1)
            pool.wait_ge(s_pos, 48)
            pool.tensor_tensor(pc[:, :], pc[:, :], bb[:, :], ALU.add).then_inc(s_pc, 1)

            def rstd_of(n):
                pool.wait_ge(s_ag, T * (n + 1))
                pool.tensor_tensor(rstd[:, :], mv[:, :, 1], eps[:, :], ALU.add).then_inc(s_ve, 1)
                pool.wait_ge(s_ve, n + 1)
                pool.tensor_tensor(rstd[:, :], rstd[:, :], half[:, :], ALU.pow).then_inc(s_rstd, 1)

            rstd_of(0)
            for i in range(NU):
                m, nh, w = unit_shape(i)
                pool.wait_ge(s_ri, i + 1)
                e = unit_tile(Eb[:, i % NE_, :], i)
                pool.tensor_tensor(e, e, rs[0:m, i % NE_, 0:nh, None].broadcast_to([m, nh, w]), ALU.mult).then_inc(s_pr, 1)
            rstd_of(1)
            pool.wait_ge(s_vrc, 2)
            for r, v in enumerate((vrow, vrev)):
                pool.dma_start(ar[B * r:B * r + B, :], v[:, :].rearrange("p (b s) -> p b s", b=B)).then_inc(s_ar, 16)
            pool.wait_ge(s_sn, 1)
            pool.dma_start(bw[:, :, :], dre[B:2 * B, :, :]).then_inc(s_bwd, 16)
            pool.wait_ge(s_z, 1)
            for r in range(2):
                pool.dma_start(feats[r:r + 1, :].rearrange("p (b s) -> p b s", b=B), ft[:, r, :]).then_inc(s_fe, 16)

        @block.scalar
        def _(act):
            act.wait_ge(s_mt, 1)
            act.activation(mTa[:, :], ps[:, 6, 0:M], ACT.Copy).then_inc(s_mtc, 1)
            act.wait_ge(s_set, 3)
            act.activation(mTb[0:DB, :], ps[0:DB, 6, 128:128 + M], ACT.Copy).then_inc(s_mtc, 1)
            act.wait_ge(s_mkv, 1)
            act.wait_ge(s_cst, 16)
            for j in range(4):
                act.activation(mkda[:, j, :], ps[:, 7, 0:M], ACT.Copy, scale=headmask[:, j:j + 1]).then_inc(s_mkc, 1)
                act.activation(mkdb[:, j, :], ps[0:DB, 7, 128:128 + M], ACT.Copy, scale=headmask[0:DB, j:j + 1]).then_inc(s_mkc, 1)
            for n in range(1, 2 * CK, 2):
                act.wait_ge(s_pt, n + 1)
                c, g = n // 2, n % 2
                act.activation(pT[:, c, :, 1:S].rearrange("p b (gh gw) -> p gw b gh", gw=GRID)[:, 3 * g:3 * g + 3],
                               ps[:, n % 4, 0:3 * B * GRID].rearrange("p (gw b gh) -> p gw b gh", gw=3, b=B),
                               ACT.Copy).then_inc(s_ptc_a, 1)
            act.wait_ge(s_xt, T)
            act.wait_ge(s_set, 2)
            act.activation(xTb[0:DB, :], psf[0:DB, 1024:1024 + N], ACT.Copy).then_inc(s_xtc, 1)
            act.wait_ge(s_q, 1)
            for j in range(2):
                act.activation(qa[:, j, 0:N].rearrange("p (a n) -> p a n", a=2), ps[:, 4:6, 0:N2], ACT.Copy, scale=halfmask[:, j:j + 1]).then_inc(s_qc, 1)
            act.wait_ge(s_q, 2)
            act.activation(qb[:, 0:N].rearrange("p (a n) -> p a n", a=2), ps[0:DB, 6:8, 0:N2], ACT.Copy).then_inc(s_qc, 1)
            act.wait_ge(s_k, 1)
            for j in range(4):
                act.activation(kda[:, j, :].rearrange("p (a n) -> p a n", a=2), ps[:, 0:2, 0:N2], ACT.Copy,
                               scale=headmask[:, j:j + 1]).then_inc(s_kc_a, 1)

            def exps(i):
                act.wait_ge(s_sub, i + 1)
                e = unit_tile(Eb[:, i % NE_, :], i)
                act.activation(e, e, ACT.Exp).then_inc(s_exp, 1)

            def copy_probs(i):
                kind, a, g = UNITS[i]
                for r in range(2 if kind == "self" else 1):
                    k = PT0[i] + r
                    act.wait_ge(s_tp, k + 1)
                    if k >= NPT:
                        act.wait_ge(s_o, max(j for j in range(NU) if PT0[j] <= k - NPT) + 1)
                    if kind == "self":
                        act.activation(PTs[0:2 * S, k % NPT, 0:3 * P], ps[0:2 * S, PT_BANK[k % 3], 0:3 * P], ACT.Copy).then_inc(s_tpc, 1)
                    else:
                        m = ROWS[a]
                        act.activation(PTs[0:M, k % NPT, :].rearrange("p (c m) -> p c m", c=4)[:, :, 0:m],
                                       ps[0:M, PT_BANK[k % 3], :].rearrange("p (c m) -> p c m", c=4)[:, :, 0:m],
                                       ACT.Copy).then_inc(s_tpc, 1)

            for i in range(NU + 1):
                if i < NU:
                    exps(i)
                if i >= 1:
                    copy_probs(i - 1)

            act.wait_ge(s_al, 1)
            act.activation(tha[:, :].rearrange("p (a n) -> p a n", a=2), ps[:, 0:2, 0:N2], ACT.Tanh, scale=0.5).then_inc(s_th, 1)
            act.wait_ge(s_al, 2)
            act.activation(thb[:, :].rearrange("p (a n) -> p a n", a=2), ps[0:DB, 2:4, 0:N2], ACT.Tanh, scale=0.5).then_inc(s_th, 1)
            act.wait_ge(s_xt, 2 * T)
            act.activation(xTb[0:DB, :], psf[0:DB, 1024:1024 + N], ACT.Copy).then_inc(s_xtc, 1)
            act.wait_ge(s_g1, 1)
            act.activation(g2[:, :], g1[:, :], ACT.Exp).then_inc(s_g2, 1)
            for e in range(E):
                for n in range(2 * FM):
                    k = 2 * FM * e + n
                    a, f = n // FM, n % FM
                    if n == 0 and e >= 2:
                        act.wait_ge(s_y, T * (e - 1))
                    act.wait_ge(s_h1, k + 1)
                    act.activation(hT[:, e % 2, f, a * N2:(a + 1) * N2], ps[:, k % 4, 0:N2], ACT.Gelu_apprx_tanh).then_inc(s_ge, 1)

        @block.vector
        def _(dve):
            dve.wait_ge(s_mkv, 2)
            dve.wait_ge(s_set, 4)
            mvv = ps[0:M, 5, 0:D].rearrange("p (j a d) -> p j a d", a=2, d=DH)
            for a in range(2):
                dve.tensor_copy(mvz[:, a::2, DH * a:DH * a + DH], mvv[:, :, a, :]).then_inc(s_mvc, 1)
            for ih in range(IH):
                dve.wait_ge(s_x[ih], 16)
                dve.tensor_copy(xp[:, :, 8 * ih:8 * ih + 8, :], xs[:, 8 * ih:8 * ih + 8, :].rearrange("p i (g j) -> p g i j", g=GW)).then_inc(s_xp, 1)
            dve.wait_ge(s_set, 10)
            for n in range(0, 2 * CK, 2):
                dve.wait_ge(s_pt, n + 1)
                c, g = n // 2, n % 2
                dve.tensor_copy(pT[:, c, :, 1:S].rearrange("p b (gh gw) -> p gw b gh", gw=GRID)[:, 3 * g:3 * g + 3],
                                ps[:, n % 4, 0:3 * B * GRID].rearrange("p (gw b gh) -> p gw b gh", gw=3, b=B)).then_inc(s_ptc_v, 1)

            def moments(n, t):
                m = ROWS[t]
                dve.wait_ge(s_h, T * n + t + 1)
                dve.bn_stats(st6[0:m, t, :], h[0:m, t, :]).then_inc(s_st, 1)
                dve.wait_ge(s_st, T * n + t + 1)
                dve.bn_aggr(mv[0:m, t, :], st6[0:m, t, :]).then_inc(s_ag, 1)

            def normalise(n):
                dve.wait_ge(s_rstd, n + 1)
                for t in range(T):
                    m = ROWS[t]
                    if n == 1 and t == 0:
                        dve.wait_ge(s_xt, T)
                    dve.tensor_scalar(xn[0:m, t, :], h[0:m, t, :], mv[0:m, t, 0:1], rstd[0:m, t:t + 1], ALU.subtract, ALU.mult).then_inc(s_xn, 1)
                dve.wait_ge(s_xt, T * (n + 1))
                dve.tensor_copy(xTa[:, :], psf[:, 0:N]).then_inc(s_xtc, 1)

            dve.wait_ge(s_set, 9)
            for t in range(T):
                m = ROWS[t]
                dve.wait_ge(s_tok, t + 1)
                dve.tensor_copy(h[0:m, t, :], ps[0:m, 4 + t % 4, 0:D]).then_inc(s_h, 1)
                moments(0, t)
            normalise(0)
            dve.wait_ge(s_xtc, 2)
            for xr, xT, r in ((xra, xTa, P), (xrb, xTb, DB + 1)):
                dve.tensor_copy(xr[:, :, :, :], xT[:, :].rearrange("p (b s) -> p b s", b=B)[:, :, None, :].broadcast_to([r, B, 2, S])).then_inc(s_xr, 1)
            dve.wait_ge(s_k, 2)
            for j in range(4):
                dve.tensor_scalar(kdb[:, j, :].rearrange("p (a n) -> p a n", a=2), ps[0:DB, 2:4, 0:N2], headmask[0:DB, j:j + 1], None, ALU.mult).then_inc(s_kc_v, 1)

            def shift(i):
                m, nh, w = unit_shape(i)
                s = unit_tile(ps[:, S_BANK[i % 2], :], i)
                dve.wait_ge(s_sc, i + 1)
                dve.tensor_reduce(mx[0:m, i % NE_, 0:nh], s, AX_X, ALU.max).then_inc(s_mx, 1)
                if i >= NE_:
                    dve.wait_ge(s_tp, PT0[i - NE_ + 1])
                dve.wait_ge(s_mx, i + 1)
                dve.tensor_tensor(unit_tile(Eb[:, i % NE_, :], i), s, mx[0:m, i % NE_, 0:nh, None].broadcast_to([m, nh, w]), ALU.subtract).then_inc(s_sub, 1)

            def sums(i):
                m, nh, w = unit_shape(i)
                dve.wait_ge(s_exp, i + 1)
                dve.tensor_reduce(sm[0:m, i % NE_, 0:nh], unit_tile(Eb[:, i % NE_, :], i), AX_X, ALU.add).then_inc(s_sum, 1)
                dve.wait_ge(s_sum, i + 1)
                dve.reciprocal(rs[0:m, i % NE_, 0:nh], sm[0:m, i % NE_, 0:nh]).then_inc(s_ri, 1)

            def mask_values(i):
                u = UNITS[i][1]
                dve.wait_ge(s_v, u + 1)
                if u >= 2:
                    dve.wait_ge(s_o, SELF[u - 2] + 1)
                dve.tensor_tensor(vbd[:, u % 2, :, :], ps[0:2 * S, V_BANK, 0:2 * D].rearrange("p (a n) -> p a n", a=2),
                                  vmask[:, None, :].broadcast_to([2 * S, 2, D]), ALU.mult).then_inc(s_vc, 1)

            def copy_heads(i):
                kind, a, g = UNITS[i]
                o = ps[:, O_BANK[i % 2], :]
                dve.wait_ge(s_o, i + 1)
                if kind == "self":
                    w = 2 * S
                    dve.tensor_copy(aTa[:, w * a:w * a + w], o[:, 0:w])
                    dve.tensor_copy(aTb[:, w * a:w * a + w], o[0:DB, 256:256 + w]).then_inc(s_oc, 1)
                else:
                    m, r = ROWS[a], 64 * (g % 2)
                    dst = mTb1 if g == 2 else mTa1
                    dve.tensor_copy(dst[r:r + 64, P * a:P * a + m], o[r:r + 64, 0:m]).then_inc(s_oc, 1)

            dve.wait_ge(s_set, 12)
            for i in range(NU + 3):
                if i < NU:
                    shift(i)
                    if UNITS[i][0] == "self":
                        mask_values(i)
                if 1 <= i <= NU:
                    sums(i - 1)
                if i >= 3:
                    copy_heads(i - 3)

            dve.wait_ge(s_oc, NU)
            parts = [(aTa[:, :], mTa1[:, :], tha[:, :], fTa[:, :]), (aTb[:, :], mTb1[0:DB, :], thb[:, :], fTb[0:DB, :])]
            dve.wait_ge(s_al, 2)
            for j, (a, a1, th, f) in enumerate(parts):
                dve.tensor_tensor(f, a, a1, ALU.add).then_inc(s_df, 1)
                dve.tensor_tensor(a, a, a1, ALU.subtract).then_inc(s_df, 1)
            for j, (a, a1, th, f) in enumerate(parts):
                dve.wait_ge(s_th, j + 1)
                dve.wait_ge(s_df, 2 * j + 2)
                dve.tensor_tensor(th, th, a, ALU.mult).then_inc(s_fu, 1)
                dve.wait_ge(s_fu, 2 * j + 1)
                dve.tensor_tensor(f, f, th, ALU.add).then_inc(s_fu, 1)
                dve.wait_ge(s_fu, 2 * j + 2)
                dve.tensor_scalar(f, f, 0.5, None, ALU.mult).then_inc(s_ft, 1)
            for t in range(T):
                m = ROWS[t]
                dve.wait_ge(s_pj, t + 1)
                dve.tensor_tensor(h[0:m, t, :], ps[0:m, 4 + t % 4, 0:D], h[0:m, t, :], ALU.add).then_inc(s_h, 1)
                moments(1, t)
            normalise(1)
            dve.wait_ge(s_vr, 1)
            dve.tensor_scalar(vrow[:, :].rearrange("p (a n) -> p a n", a=2), ps[0:1, 4:6, 0:N2], -3.0, 3.0, ALU.max, ALU.min).then_inc(s_vrc, 1)
            dve.wait_ge(s_vrc, 1)
            dve.tensor_copy(vrev[:, :].rearrange("p (b s) -> p b s", b=B), vrow[:, :].rearrange("p (b s) -> p b s", b=B)[:, :, ::-1]).then_inc(s_vrc, 1)
            dve.wait_ge(s_gt, 1)
            for t in range(T):
                m = ROWS[t]
                dve.tensor_copy(lg[0:m, t, :], ps[0:m, 6, 8 * t:8 * t + 8]).then_inc(s_lg, 1)
            for t in range(T):
                dve.wait_ge(s_lg, t + 1)
                dve.max(m8[:, t, :], lg[:, t, :]).then_inc(s_tk, 1)
                dve.wait_ge(s_tk, 2 * t + 1)
                dve.max_index(i8[:, t, :], m8[:, t, :], lg[:, t, :]).then_inc(s_tk, 1)
            dve.wait_ge(s_tk, 2 * T)
            dve.tensor_tensor(g1[:, :], m8[:, :, 1], m8[:, :, 0], ALU.subtract).then_inc(s_g1, 1)
            dve.tensor_copy(i8f[:, :, :], i8[:, :, 0:2]).then_inc(s_tk, 1)
            dve.wait_ge(s_tk, 2 * T + 1)
            io = iota8[:, None, :].broadcast_to([P, T, E])
            dve.tensor_tensor(comb[:, :, :], i8f[:, :, 0:1].broadcast_to([P, T, E]), io, ALU.is_equal).then_inc(s_tk, 1)
            dve.tensor_tensor(comb1[:, :, :], i8f[:, :, 1:2].broadcast_to([P, T, E]), io, ALU.is_equal).then_inc(s_tk, 1)
            dve.wait_ge(s_g2, 1)
            dve.tensor_scalar(c1[:, :], g2[:, :], 1.0, None, ALU.add).then_inc(s_tk, 1)
            dve.wait_ge(s_tk, 2 * T + 4)
            dve.reciprocal(c0[:, :], c1[:, :]).then_inc(s_tk, 1)
            dve.wait_ge(s_tk, 2 * T + 5)
            dve.tensor_tensor(c1[:, :], g2[:, :], c0[:, :], ALU.mult).then_inc(s_tk, 1)
            dve.tensor_tensor(comb[:, :, :], comb[:, :, :], c0[:, :, None].broadcast_to([P, T, E]), ALU.mult).then_inc(s_tk, 1)
            dve.wait_ge(s_tk, 2 * T + 7)
            dve.tensor_tensor(comb1[:, :, :], comb1[:, :, :], c1[:, :, None].broadcast_to([P, T, E]), ALU.mult).then_inc(s_tk, 1)
            dve.wait_ge(s_tk, 2 * T + 8)
            dve.tensor_tensor(comb[:, :, :], comb[:, :, :], comb1[:, :, :], ALU.add).then_inc(s_tk, 1)
            dve.wait_ge(s_tk, 2 * T + 9)

            def add_expert(e):
                for t in range(T):
                    m, k = ROWS[t], T * e + t
                    dve.wait_ge(s_y, k + 1)
                    if e:
                        dve.wait_ge(s_ac, k - T + 1)
                    dve.scalar_tensor_tensor(out=acc[0:m, t, :], in0=ps[0:m, 4 + k % 3, 0:D], scalar=comb[0:m, t, e:e + 1],
                                             in1=acc[0:m, t, :] if e else h[0:m, t, :], op0=ALU.mult, op1=ALU.add).then_inc(s_ac, 1)

            add_expert(0)
            dve.wait_ge(s_ar, 32)
            step = [0]

            def link(ins):
                step[0] += 1
                ins.then_inc(s_sv, 1)
                dve.wait_ge(s_sv, step[0])

            link(dve.tensor_scalar(ar[:, :], ar[:, :], -2.0, None, ALU.add))
            link(dve.tensor_tensor(asg[:, :], ar[:, :], altn[:, :], ALU.mult))
            dve.tensor_copy(dre[:, 0, 1:2], one32[:, :])
            link(dve.tensor_copy(dre[:, 0, 0:1], asg[:, 0:1]))
            for n in range(1, S):
                link(dve.tensor_tensor(dsq[:, :], dre[:, n - 1, :], dre[:, n - 1, :], ALU.mult))
                link(dve.tensor_reduce(dn[:, :], dsq[:, :], AX_X, ALU.add))
                link(dve.reciprocal(dri[:, :], dn[:, :]))
                dve.tensor_scalar(dre[:, n, 0:1], dre[:, n - 1, 0:1], dri[:, 0:1], asg[:, n:n + 1], ALU.mult, ALU.add)
                link(dve.tensor_scalar(dre[:, n, 1:2], dre[:, n - 1, 1:2], dri[:, 0:1], 1.0, ALU.mult, ALU.add))
            dve.tensor_tensor(dre[:, :, 0], dre[:, :, 0], altn[:, :], ALU.mult).then_inc(s_sn, 1)
            dve.wait_ge(s_bwd, 16)
            rev = bw[:, ::-1, :]
            link(dve.tensor_tensor(z[:, :, :], dre[0:B, :, :], rev, ALU.add))
            link(dve.tensor_tensor(z[:, :, 0], z[:, :, 0], ar[0:B, :], ALU.subtract))
            link(dve.tensor_scalar(z[:, :, 1], z[:, :, 1], -1.0, None, ALU.add))
            link(dve.tensor_tensor(zz[:, :, :], z[:, :, :], z[:, :, :], ALU.mult))
            link(dve.tensor_reduce(zn[:, :], zz[:, :, :], AX_X, ALU.add))
            link(dve.reciprocal(zr[:, :], zn[:, :]))
            link(dve.tensor_tensor(ft[:, :, :], z[:, :, :].rearrange("p s c -> p c s"), zr[:, None, :].broadcast_to([B, 2, S]), ALU.mult))
            dve.tensor_scalar(ft[:, :, :], ft[:, :, :], -10.0, 10.0, ALU.max, ALU.min).then_inc(s_z, 1)
            dve.wait_ge(s_ow, 80)
            dve.tensor_tensor(ow[:, :], ow[:, :], bk[:, :], ALU.mult).then_inc(s_owb, 1)
            for e in range(1, E):
                add_expert(e)
            for t in range(T):
                m = ROWS[t]
                dve.wait_ge(s_y, T * E + t + 1)
                dve.wait_ge(s_ac, T * E)
                dve.tensor_tensor(acc[0:m, t, :], ps[0:m, 4 + (T * E + t) % 3, 0:D], acc[0:m, t, :], ALU.add).then_inc(s_ac, 1)

        @block.tensor
        def _(pe):
            pe.wait_ge(s_cst, 16)
            pe.wait_ge(s_mem, 64)
            pe.transpose(ps[:, 6, 0:M], mf[:, 0:P], ident[0:M, 0:M])
            pe.transpose(ps[0:DB, 6, 128:128 + M], mf[:, P:D], ident[0:M, 0:M]).then_inc(s_mt, 1)
            pe.wait_ge(s_mtc, 2)
            pe.matmul(ps[:, 7, 0:M], wma[:, 0:P], mTa[:, :], start=True, stop=False)
            pe.matmul(ps[:, 7, 0:M], wmb[:, 0:P], mTb[:, :], start=False, stop=True)
            pe.matmul(ps[0:DB, 7, 128:128 + M], wma[:, P:D], mTa[:, :], start=True, stop=False)
            pe.matmul(ps[0:DB, 7, 128:128 + M], wmb[:, P:D], mTb[:, :], start=False, stop=True).then_inc(s_mkv, 1)
            pe.matmul(ps[0:M, 5, 0:D], mTa[:, :], wma[:, D:2 * D], start=True, stop=False)
            pe.matmul(ps[0:M, 5, 0:D], mTb[:, :], wmb[:, D:2 * D], start=False, stop=True).then_inc(s_mkv, 1)
            for n in range(2 * CK):
                c, g = n // 2, n % 2
                if n >= 4:
                    if n % 2:
                        pe.wait_ge(s_ptc_a, (n - 4) // 2 + 1)
                    else:
                        pe.wait_ge(s_ptc_v, (n - 4) // 2 + 1)
                pe.wait_ge(s_xp, c // (CK // IH) + 1)
                for a in range(3):
                    patch = xp[:, 3 * g + a, :, :].rearrange("p i j -> p (i j)")
                    ins = pe.transpose(ps[:, n % 4, a * 96:a * 96 + 96], patch[:, P * c:P * c + P], ident[0:96, 0:96])
                ins.then_inc(s_pt, 1)
            pe.wait_ge(s_sel, 1)
            pe.wait_ge(s_pc, 1)
            pe.wait_ge(s_wt, 16)
            pe.wait_ge(s_mvc, 2)
            pe.wait_ge(s_mkc, 8)
            pe.wait_ge(s_ptc_a, CK)
            pe.wait_ge(s_ptc_v, CK)
            self_ = sel[:, :, :].rearrange("p b s -> p (b s)")
            for t in range(T):
                m = ROWS[t]
                if t >= 4:
                    pe.wait_ge(s_h, t - 3)
                o = ps[0:m, 4 + t % 4, 0:D]
                pe.matmul(o, self_[:, P * t:P * t + m], pc[:, :], start=True, stop=False)
                for c in range(CK):
                    ins = pe.matmul(o, pT[:, c, :, :].rearrange("p b s -> p (b s)")[:, P * t:P * t + m], wt[:, c, :],
                                    start=False, stop=(c == CK - 1))
                ins.then_inc(s_tok, 1)

            def to_features(n):
                for t in range(T):
                    m = ROWS[t]
                    pe.wait_ge(s_xn, T * n + t + 1)
                    pe.transpose(psf[:, P * t:P * t + m], xn[0:m, t, 0:P], ident[0:m, 0:m])
                    pe.transpose(psf[0:DB, 1024 + P * t:1024 + P * t + m], xn[0:m, t, P:D], ident[0:m, 0:m]).then_inc(s_xt, 1)

            to_features(0)
            pe.wait_ge(s_xtc, 2)
            pe.wait_ge(s_wat, 48)

            def project(c0_, m, b0):
                for a in range(2):
                    n = slice(a * N2, (a + 1) * N2)
                    pe.matmul(ps[0:m, b0 + a, 0:N2], waa[:, c0_:c0_ + m], xTa[:, n], start=True, stop=False)
                    ins = pe.matmul(ps[0:m, b0 + a, 0:N2], wab[:, c0_:c0_ + m], xTb[:, n], start=False, stop=True)
                return ins

            project(D, DA, 0).then_inc(s_k, 1)
            project(0, DA, 4).then_inc(s_q, 1)
            project(D + DA, DB, 2).then_inc(s_k, 1)
            project(DA, DB, 6).then_inc(s_q, 1)
            pe.wait_ge(s_qc, 3)
            pe.wait_ge(s_kc_a, 4)
            pe.wait_ge(s_kc_v, 4)
            pe.wait_ge(s_xr, 2)

            def scores(i):
                kind, a, g = UNITS[i]
                s = ps[:, S_BANK[i % 2], :]
                if i >= 2:
                    pe.wait_ge(s_sub, i - 1)
                if kind == "self":
                    for r in range(2):
                        n0 = (2 * a + r) * S
                        for g in range(3):
                            q, kd = (qb, kdb) if g == 2 else (qa[:, g, :], kda)
                            ins = pe.matmul(s[64 * r:64 * r + 64, 4 * S * g:4 * S * (g + 1)], q[:, n0:n0 + 64],
                                            kd[:, :, n0:n0 + S], start=True, stop=True)
                else:
                    m = ROWS[a]
                    q, kd = (qb, mkdb) if g == 2 else (qa[:, g, :], mkda)
                    ins = pe.matmul(s[0:m, 0:4 * M], q[:, P * a:P * a + m], kd[:, :, :], start=True, stop=True)
                ins.then_inc(s_sc, 1)

            def values(i):
                u = UNITS[i][1]
                if u >= 1:
                    pe.wait_ge(s_vc, u)
                for r in range(2):
                    o = ps[0:2 * S, V_BANK, D * r:D * (r + 1)]
                    pe.matmul(o, xra[:, 2 * u + r, :, :], waa[:, 2 * D:3 * D], start=True, stop=False)
                    ins = pe.matmul(o, xrb[:, 2 * u + r, :, :], wab[:, 2 * D:3 * D], start=False, stop=True)
                ins.then_inc(s_v, 1)

            def transposes(i):
                kind, a, g = UNITS[i]
                e = Eb[:, i % NE_, :]
                pe.wait_ge(s_pr, i + 1)
                for r in range(2 if kind == "self" else 1):
                    k = PT0[i] + r
                    if k >= 3:
                        pe.wait_ge(s_tpc, k - 2)
                    o = ps[:, PT_BANK[k % 3], :]
                    if kind == "self":
                        for c in range(3):
                            h0 = 2 * (3 * r + c) * S
                            ins = pe.transpose(o[0:2 * S, P * c:P * c + P], e[:, h0:h0 + 2 * S], ident)
                    else:
                        m = ROWS[a]
                        for c in range(4):
                            ins = pe.transpose(o[0:M, P * c:P * c + m], e[0:m, c * M:(c + 1) * M], ident[0:m, 0:m])
                    ins.then_inc(s_tp, 1)

            def heads(i):
                kind, a, g = UNITS[i]
                o = ps[:, O_BANK[i % 2], :]
                if i >= 2:
                    pe.wait_ge(s_oc, i - 1)
                if kind == "self":
                    pe.wait_ge(s_tpc, PT0[i] + 2)
                    pe.wait_ge(s_vc, a + 1)
                    for c in range(6):
                        pt = PTs[0:2 * S, (PT0[i] + c // 3) % NPT, P * (c % 3):P * (c % 3) + P]
                        for r in range(2):
                            c0_ = (c // 4) * 256 + r * S
                            ins = pe.matmul(o[32 * (c % 4):32 * (c % 4) + 32, c0_:c0_ + S], vbd[:, a % 2, r, 32 * c:32 * c + 32],
                                            pt[:, 64 * r:64 * r + S], start=True, stop=True)
                else:
                    pe.wait_ge(s_tpc, PT0[i] + 1)
                    m = ROWS[a]
                    pt = PTs[0:M, PT0[i] % NPT, :]
                    for c in range(4):
                        p0 = 64 * (g % 2) + 32 * (c // 2)
                        ins = pe.matmul(o[p0:p0 + 32, 0:m], mvz[:, 4 * g + c, :], pt[:, P * c:P * c + m], start=(c % 2 == 0), stop=(c % 2 == 1))
                ins.then_inc(s_o, 1)

            for i in range(NU + 3):
                if i < NU:
                    scores(i)
                    if UNITS[i][0] == "self":
                        values(i)
                if 1 <= i <= NU:
                    transposes(i - 1)
                if 2 <= i <= NU + 1:
                    heads(i - 2)

            pe.wait_ge(s_wal, 128)
            pe.wait_ge(s_oc, NU)
            for c0_, m, b0 in ((0, DA, 0), (DA, DB, 2)):
                for a in range(2):
                    n = slice(a * N2, (a + 1) * N2)
                    o = ps[0:m, b0 + a, 0:N2]
                    pe.matmul(o, wal[:, 0, c0_:c0_ + m], aTa[:, n], start=True, stop=False)
                    pe.matmul(o, wal[0:DB, 1, c0_:c0_ + m], aTb[:, n], start=False, stop=False)
                    pe.matmul(o, wal[:, 2, c0_:c0_ + m], mTa1[:, n], start=False, stop=False)
                    ins = pe.matmul(o, wal[0:DB + 1, 3, c0_:c0_ + m], mTb1[:, n], start=False, stop=True)
                ins.then_inc(s_al, 1)
            pe.wait_ge(s_ft, 2)
            for t in range(T):
                m = ROWS[t]
                if t >= 4:
                    pe.wait_ge(s_h, T + t - 3)
                o = ps[0:m, 4 + t % 4, 0:D]
                pe.matmul(o, fTa[:, P * t:P * t + m], wpa[:, :], start=True, stop=False)
                pe.matmul(o, fTb[:, P * t:P * t + m], wpb[:, :], start=False, stop=True).then_inc(s_pj, 1)
            to_features(1)
            pe.wait_ge(s_gw, 96)
            pe.wait_ge(s_xtc, 4)
            for a in range(2):
                n = slice(a * N2, (a + 1) * N2)
                pe.matmul(ps[0:1, 4 + a, 0:N2], vwa[:, :], xTa[:, n], start=True, stop=False)
                ins = pe.matmul(ps[0:1, 4 + a, 0:N2], vwb[:, :], xTb[:, n], start=False, stop=True)
            ins.then_inc(s_vr, 1)
            for t in range(T):
                m = ROWS[t]
                n = slice(P * t, P * t + m)
                pe.matmul(ps[0:m, 6, 8 * t:8 * t + 8], xTa[:, n], gva[:, :], start=True, stop=False)
                ins = pe.matmul(ps[0:m, 6, 8 * t:8 * t + 8], xTb[:, n], gvb[:, :], start=False, stop=True)
            ins.then_inc(s_gt, 1)

            def hidden(e):
                w = e % 2
                pe.wait_ge(s_w[w], 80 * (e // 2 + 1))
                for n in range(2 * FM):
                    k = 2 * FM * e + n
                    a, f = n // FM, n % FM
                    if k >= 4:
                        pe.wait_ge(s_ge, k - 3)
                    o = ps[:, k % 4, 0:N2]
                    cols = slice(a * N2, (a + 1) * N2)
                    pe.matmul(o, W1A[:, w, P * f:P * f + P], xTa[:, cols], start=True, stop=False)
                    pe.matmul(o, W1B[:, w, P * f:P * f + P], xTb[:, cols], start=False, stop=True).then_inc(s_h1, 1)

            def outputs(e):
                w = e % 2
                pe.wait_ge(s_ge, 2 * FM * (e + 1))
                for t in range(T):
                    k = T * e + t
                    m = ROWS[t]
                    if k >= 3:
                        pe.wait_ge(s_ac, k - 2)
                    o = ps[0:m, 4 + k % 3, 0:D]
                    for f in range(FM):
                        pe.matmul(o, hT[:, w, f, P * t:P * t + m], W2[:, w, f, :], start=(f == 0), stop=False)
                    pe.matmul(o, ones[:, 0:m], B2[:, w, :], start=False, stop=True).then_inc(s_y, 1)

            for e in range(E):
                hidden(e)
                if e == 0:
                    pe.wait_ge(s_vrc, 1)
                    pe.wait_ge(s_lg, T)
                if e >= 1:
                    outputs(e - 1)
            outputs(E - 1)
            pe.wait_ge(s_owb, 1)
            pe.wait_ge(s_fe, 32)
            for t in range(T):
                k = T * E + t
                m = ROWS[t]
                pe.wait_ge(s_ac, k - 2)
                pe.matmul(ps[0:m, 4 + k % 3, 0:D], feats[:, P * t:P * t + m], ow[:, :], start=True, stop=True).then_inc(s_y, 1)


_INS = ["x", "cls_tok", "L0_tok_W", "L0_tok_b", "L0_tok_pos_emb", "L0_attn_w_attn", "L0_attn_b_attn", "L0_attn_w_proj",
        "L0_attn_b_proj", "L0_attn_w_mem", "L0_attn_b_mem", "L0_attn_w_alpha", "L0_attn_b_alpha", "L0_attn_memory_features",
        "L0_ffn_v_w", "L0_ffn_v_b", "L0_ffn_gate_w", "L0_ffn_gate_b", "L0_ffn_w1", "L0_ffn_b1", "L0_ffn_w2", "L0_ffn_b2",
        "L0_ffn_out_w", "L0_ffn_out_b", "L0_ffn_bk_scale"]


def kernel(**inputs):
    import numpy as _np
    import concourse.bacc as _bacc
    from concourse import mybir as _mybir
    from concourse.bass_utils import run_bass_kernel_spmd as _run

    nc = _bacc.Bacc("TRN2", target_bir_lowering=False, num_devices=1)
    arrays, args = {}, []
    for name in _INS:
        a = _np.ascontiguousarray(inputs[name])
        if a.ndim == 0:
            a = a.reshape(1, 1)
        arrays[f"in_{name}"] = a
        args.append(nc.dram_tensor(f"in_{name}", a.shape, _mybir.dt.from_np(a.dtype), kind="ExternalInput").ap())
    p = _np.arange(128)[:, None]
    ident = p == _np.arange(128)[None]
    headmask = (p // 16) % 4 == _np.arange(4)[None]
    vmask = p // 37 == (_np.arange(192)[None] // 16) % 2
    iota8 = _np.arange(8)[None] + 0 * p
    halfmask = p // 64 == _np.arange(2)[None]
    consts = _np.concatenate([ident, headmask, vmask, iota8, halfmask], axis=1).astype(_np.float32)
    arrays["in_consts"] = consts
    args.append(nc.dram_tensor("in_consts", consts.shape, _mybir.dt.float32, kind="ExternalInput").ap())
    args.append(nc.dram_tensor("out_0", (16, 37, 192), _mybir.dt.float32, kind="ExternalOutput").ap())
    vit_block(nc, *args)
    r = _run(nc, [arrays], core_ids=[0])
    return r.results[0]["out_0"]
```

```python
from contextlib import ExitStack

import concourse.bass as bass
from concourse import mybir

ALU = mybir.AluOpType
ACT = mybir.ActivationFunctionType
F32 = mybir.dt.float32
U32 = mybir.dt.uint32
I32 = mybir.dt.int32
BF16 = mybir.dt.bfloat16
AX_X = mybir.AxisListType.X

P = 128


CONSTS = (("ident", 128), ("headmask", 6), ("vmask", 192), ("iota", 8), ("blocks_from", 5), ("earlier", 64),
          ("block", 17), ("no_token", 5), ("before", 128), ("alternate", 37))


def vit_block(nc, x, cls_tok, tok_w, tok_b, pos_emb, w_attn, b_attn, w_proj, b_proj, w_mem, b_mem, w_alpha, b_alpha,
              memory, v_w, v_b, gate_w, gate_b, w1, b1, w2, b2, out_w, out_b, bk_scale, consts, out):
    B, IMG, _, CH = x.shape
    PDIM, D = tok_w.shape
    GRID = 6
    PATCH = IMG // GRID
    NP_ = GRID * GRID
    S = NP_ + 1
    N = B * S
    N2 = N // 2
    NH, DH = 12, 16
    M = memory.shape[1]
    E, _, F = w1.shape
    H = D // 2
    HH = NH // 2
    T = -(-N // P)
    ROWS = [min(P, N - P * t) for t in range(T)]
    ROW = CH * PATCH
    IH = 2
    CK = PDIM // P
    GW = GRID
    NB = (2 * N - E) // P + E
    NW = 3
    FM = F // P
    U = B // 2

    with ExitStack() as ctx:
        def sb(name, shape, dt=F32):
            return ctx.enter_context(nc.sbuf_tensor(name, shape, dt))

        def sem(name):
            return ctx.enter_context(nc.semaphore(name))

        ps = ctx.enter_context(nc.psum_tensor("ps", [P, 8, 512], F32))
        psf = ps[:, :, :].rearrange("p a b -> p (a b)")

        at = 0
        named = {}
        for name, width in CONSTS:
            named[name] = (at, at + width)
            at += width
        cst = sb("cst", [P, at])

        def const(name, rows=P):
            return cst[0:rows, named[name][0]:named[name][1]]

        ident = const("ident")
        headmask = const("headmask")
        vmask = const("vmask")

        early = sb("early", [P, 2 * PATCH * IMG * CH])
        xs = early[0:B * GRID, 0:PATCH * IMG * CH].rearrange("p (i j) -> p i j", i=PATCH)
        xp = early[0:B * GRID, PATCH * IMG * CH:].rearrange("p (g i j) -> p g i j", g=GW, i=PATCH)
        wt = sb("wt", [P, CK, D])
        pT = sb("pT", [P, CK, B, S])
        sel = sb("sel", [S, B, S])
        pc = sb("pc", [S, D])
        bb = sb("bb", [S, D])
        h = sb("h", [P, T, D])
        xn = sb("xn", [P, T, D])
        st6 = sb("st6", [P, T, 6])
        mv = sb("mv", [P, T, 2])
        eps = sb("eps", [P, T])
        half = sb("half", [P, T])
        rstd = sb("rstd", [P, T])
        xT = sb("xT", [P, 2, N])
        XR = B * 2 * S
        xrf = sb("xr", [P, 2 * XR + P])
        xr = xrf[:, 0:2 * XR].rearrange("p (m b r s) -> p m b r s", m=2, b=B, r=2)
        wsb = sb("wsb", [P, 16 * D + 2 * E + 2])
        wcol = [0]

        def weights(halves, n):
            c = wcol[0]
            wcol[0] += halves * n
            return wsb[:, c:c + halves * n].rearrange("p (a n) -> p a n", a=halves)

        wm = weights(2, 2 * D)
        wa = weights(2, 3 * D)
        wal = weights(4, D)
        wp = weights(2, D)
        gv = weights(2, E)
        vw = weights(2, 1)
        q = sb("q", [P, 2, N + 64])
        mid = sb("mid", [P, 2 * HH * N])
        kd = mid[:, :].rearrange("p (m j n) -> p m j n", m=2, j=HH)
        xg = mid[:, 0:NB * D].rearrange("p (b n) -> p b n", b=NB)
        mf = sb("mf", [M, D])
        mT = sb("mT", [P, 2, M])
        mkd = sb("mkd", [P, 2, HH, M])
        mvz = sb("mvz", [P, NH, 32])
        NE_ = 4
        Eb = sb("Eb", [P, NE_, 512])
        mx = sb("mx", [P, NE_, NH])
        sm = sb("sm", [P, NE_, NH])
        rs = sb("rs", [P, NE_, NH])
        NPT = 3
        PTs = sb("PTs", [P, NPT, 512])
        vbd = sb("vbd", [P, 2, 2, D])
        aT = sb("aT", [P, 2, N])
        a1T = sb("a1T", [P, 2, N])
        th = sb("th", [H, 2, N])
        fT = sb("fT", [P, 2, N])
        lg = sb("lg", [P, T, E])
        m8 = sb("m8", [P, T, 8])
        i8 = sb("i8", [P, T, 8], U32)
        i8f = sb("i8f", [P, T, 2])
        g1 = sb("g1", [P, T])
        g2 = sb("g2", [P, T])
        c0 = sb("c0", [P, T])
        c1 = sb("c1", [P, T])
        oh = sb("oh", [P, 2, T, E])
        ohs = sb("ohs", [P, T + 1, E], BF16)
        trib = sb("trib", [P, P], BF16)
        oneb = sb("oneb", [P, P], BF16)
        cmp5 = sb("cmp5", [P, E, T])
        nblk = sb("nblk", [P, E])
        cmp8 = sb("cmp8", [P, E, E])
        base = sb("base", [P, E])
        cend = sb("cend", [P, E])
        cmpb = sb("cmpb", [1, NB, E])
        ebf = sb("ebf", [1, NB])
        ebi = sb("ebi", [1, NB], I32)
        rb = sb("rb", [P, T, E])
        sl3 = sb("sl3", [P, 2, T, E])
        slf = sb("slf", [P, 2, T])
        sli = sb("sli", [P, 2, T], U32)
        zero = sb("zero", [P, D])
        comb = sb("comb", [P, 2, T, E])
        vrow = sb("vrow", [1, N])
        vrev = sb("vrev", [1, N])
        ar = sb("ar", [2 * B, S])
        asg = sb("asg", [2 * B, S])
        dre = sb("dre", [2 * B, S, 2])
        dsq = sb("dsq", [2 * B, 2])
        dn = sb("dn", [2 * B, 1])
        dri = sb("dri", [2 * B, 1])
        one32 = sb("one32", [2 * B, 1])
        bw = sb("bw", [B, S, 2])
        z = sb("z", [B, S, 2])
        zz = sb("zz", [B, S, 2])
        zn = sb("zn", [B, S])
        zr = sb("zr", [B, S])
        ft = sb("ft", [B, 2, S])
        R = E + 3
        feats = sb("feats", [R, N])
        ow = sb("ow", [R, D])
        bk = sb("bk", [R, D])
        W1 = early[:, 0:NW * 2 * F].rearrange("p (w a f) -> p w a f", w=NW, a=2)
        W2 = early[:, NW * 2 * F:NW * 2 * F + NW * FM * D].rearrange("p (w m n) -> p w m n", w=NW, m=FM)
        XT = sb("XT", [P, 2, 2, P])
        hT = sb("hT", [P, 2, FM, P])
        ysb = sb("ysb", [P, 3, D])
        acc = sb("acc", [P, T, D])
        yg = pT[:, :, :, :].rearrange("p c b s -> p (c b s)")[:, 0:2 * T * D].rearrange("p (k t n) -> p k t n", k=2, t=T)
        xs_dram = nc.dram_tensor("slots_in", [NB * P, D], F32).ap()
        ys_dram = nc.dram_tensor("slots_out", [NB * P, D], F32).ap()

        s_cst = sem("consts_landed")
        s_x = [sem(f"image_rows_landed{i}") for i in range(IH)]
        s_wt = sem("patch_weights_landed")
        s_pos = sem("positions_landed")
        s_mem = sem("memory_landed")
        s_wat = sem("attn_weights_landed")
        s_wal = sem("alpha_weights_landed")
        s_gw = sem("gate_weights_landed")
        s_ow = sem("spec_weights_landed")
        s_set = sem("pool_setup")
        s_wz = sem("weight_rows_cleared")
        s_w1z = sem("expert_weight_rows_cleared")
        s_sel = sem("selector_ready")
        s_pc = sem("positions_ready")
        s_mt = sem("memory_transposed")
        s_mtc = sem("memory_transposed_copied")
        s_mkv = sem("memory_kv_ready")
        s_mkc = sem("memory_keys_spread")
        s_mvc = sem("memory_values_spread")
        s_xp = sem("patch_rows_gathered")
        s_xr = sem("tokens_repeated")
        s_pt = sem("patches_transposed")
        s_ptc_a = sem("patches_copied_by_act")
        s_ptc_v = sem("patches_copied_by_dve")
        s_tok = sem("tokens_summed")
        s_h = sem("tokens_copied")
        s_st = sem("moments_taken")
        s_ag = sem("mean_and_variance")
        s_ve = sem("variance_plus_eps")
        s_rstd = sem("rstd_ready")
        s_xn = sem("tokens_normalised")
        s_xt = sem("tokens_transposed")
        s_xtc = sem("tokens_transposed_copied")
        s_q = sem("queries_summed")
        s_qc = sem("queries_copied")
        s_k = sem("keys_summed")
        s_kc_a = sem("keys_spread_by_act")
        s_kc_v = sem("keys_spread_by_dve")
        s_v = sem("values_summed")
        s_vc = sem("values_masked")
        s_sc = sem("scores_ready")
        s_mx = sem("score_maxima")
        s_sub = sem("scores_shifted")
        s_exp = sem("exps_ready")
        s_sum = sem("exp_sums")
        s_ri = sem("sum_reciprocals")
        s_pr = sem("probs_ready")
        s_tp = sem("probs_transposed")
        s_tpc = sem("probs_transposed_copied")
        s_o = sem("heads_summed")
        s_oc = {kind: sem(f"heads_copied_{kind}") for kind in ("self", "mem")}
        s_al = sem("alpha_summed")
        s_th = sem("tanh_ready")
        s_df = sem("differences_ready")
        s_fu = sem("fused_products")
        s_ft = sem("fused_ready")
        s_pj = sem("projection_summed")
        s_gt = sem("gates_summed")
        s_vr = sem("potentials_summed")
        s_vrc = sem("potentials_clipped")
        s_lg = sem("logits_copied")
        s_tk = sem("top2_steps")
        s_g1 = sem("gate_differences")
        s_g2 = sem("gate_exps")
        s_ar = sem("scan_inputs_landed")
        s_sn = sem("scan_steps_pool")
        s_sv = sem("scan_steps_dve")
        s_bwd = sem("backward_landed")
        s_z = sem("green_steps")
        s_fe = sem("features_landed")
        s_owb = sem("spec_weights_scaled")
        s_lgz = sem("route_steps")
        s_rt = sem("ranks_summed")
        s_eb = sem("block_experts_ready")
        s_sl = sem("slots_ready")
        s_cb = sem("shares_ready")
        s_ct = sem("shares_transposed")
        s_ctc = sem("shares_copied")
        s_b2 = sem("bias_rows_landed")
        s_zs = sem("slots_cleared")
        s_sct = sem("tokens_scattered")
        s_w = [sem(f"expert_weights_landed{i}") for i in range(NW)]
        s_xg = [sem(f"block_tokens_landed{i}") for i in range(2)]
        s_bt = sem("block_transposed")
        s_btc = sem("block_transposed_copied")
        s_h1 = sem("hidden_summed")
        s_ge = sem("gelu_ready")
        s_y = sem("block_out_summed")
        s_yc = sem("block_out_copied")
        s_yo = [sem(f"block_out_written{i}") for i in range(3)]
        s_sp = sem("spectral_summed")
        s_ba = sem("residual_ready")
        s_gg = [sem(f"outputs_gathered{i}") for i in range(2)]
        s_fin = sem("outputs_blended")
        s_out = sem("out_written")

        block = ctx.enter_context(nc.Block())

        UNITS = []
        for u in range(U):
            UNITS.append(("self", u, 0))
            UNITS += [("mem", *divmod(j, 3)) for j in range(2 * u, min(2 * u + 2, 3 * T))]
        NU = len(UNITS)
        PT0 = []
        k = 0
        for kind, _, _ in UNITS:
            PT0.append(k)
            k += 2 if kind == "self" else 1
        SELF = [i for i in range(NU) if UNITS[i][0] == "self"]
        assert sum(1 for kind, _, _ in UNITS if kind == "mem") == 3 * T
        S_BANK, PT_BANK, O_BANK, V_BANK = [0, 1], [2, 3, 4], {"self": 5, "mem": 6}, 7

        LAG_PROBS, LAG_HEADS = 2, 3

        def unit_shape(i):
            kind, a, _ = UNITS[i]
            return (P, NH, S) if kind == "self" else (ROWS[a], 4, M)

        def unit_tile(buf, i):
            m, nh, w = unit_shape(i)
            return buf[0:m, 0:nh * w].rearrange("p (h w) -> p h w", h=nh)

        @block.sync
        def _(sp):
            xv = x.rearrange("b (g i) j c -> (b g) i (j c)", i=PATCH)
            sp.dma_start(cst[:, :], consts).then_inc(s_cst, 16)
            for ih in range(IH):
                sp.dma_start(xs[:, 8 * ih:8 * ih + 8, :], xv[:, 8 * ih:8 * ih + 8, :]).then_inc(s_x[ih], 16)
            sp.dma_start(wt[:, :, :], tok_w.rearrange("(c p) n -> p c n", p=P)).then_inc(s_wt, 16)

            def halves(dst, src, s):
                sp.dma_start(dst, src.rearrange("(a p) n -> p a n", p=H)).then_inc(s, 16)

            def row(dst, src, s):
                sp.dma_start(dst, src.rearrange("(a n) -> a n", a=1)).then_inc(s, 16)

            halves(wa[0:H, :, :], w_attn, s_wat)
            sp.wait_ge(s_wz, 1)
            row(wa[H:H + 1, 1, :], b_attn, s_wat)
            halves(wal[0:H, :, :], w_alpha, s_wal)
            row(wal[H:H + 1, 3, :], b_alpha, s_wal)
            halves(wp[0:H, :, :], w_proj, s_wal)
            row(wp[H:H + 1, 1, :], b_proj, s_wal)
            halves(gv[0:H, :, :], gate_w, s_gw)
            row(gv[H:H + 1, 1, :], gate_b, s_gw)
            for m in range(2):
                sp.dma_start(vw[0:H, m, :], v_w.rearrange("(p a) -> p a", a=1)[H * m:H * m + H]).then_inc(s_gw, 16)
            sp.dma_start(vw[H:H + 1, 1, :], v_b).then_inc(s_gw, 16)
            sp.dma_start(ow[0:E, :], b2).then_inc(s_ow, 16)
            sp.dma_start(ow[E:E + 2, :], out_w).then_inc(s_ow, 16)
            row(ow[E + 2:E + 3, :], out_b, s_ow)
            sp.wait_ge(s_set, 11)
            sp.dma_start(bk[E:R, :], bk_scale.rearrange("(a n) -> a n", a=1).broadcast_to([3, D])).then_inc(s_ow, 16)

            def load_weights(b):
                w = b % NW
                e = nc.sync.value_load(ebi[0:1, b:b + 1], min_val=0, max_val=E - 1)
                if b >= NW:
                    sp.wait_ge(s_y, b - NW + 1)
                sp.dma_start(W1[0:H, w, :, :], w1[bass.DynSlice(e, 1)].rearrange("e (a p) f -> p (e a) f", p=H)).then_inc(s_w[w], 16)
                sp.dma_start(W1[H:H + 1, w, 1, :], b1[bass.DynSlice(e, 1)]).then_inc(s_w[w], 16)
                sp.dma_start(W2[:, w, :, :], w2[bass.DynSlice(e, 1)].rearrange("e (m p) n -> p (e m) n", p=P)).then_inc(s_w[w], 16)

            def store_outputs(b):
                sp.wait_ge(s_yc, b + 1)
                sp.dma_start(ys_dram[P * b:P * b + P, :], ysb[:, b % 3, :]).then_inc(s_yo[b % 3], 16)

            sp.wait_ge(s_eb, 1)
            sp.wait_ge(s_w1z, 1)
            for b in range(3):
                load_weights(b)
            sp.wait_ge(s_sct, 16 * 2 * T)
            for n, (b0, b1_) in enumerate(((0, 2), (2, NB))):
                sp.dma_start(xg[:, b0:b1_, :], xs_dram[P * b0:P * b1_, :].rearrange("(b p) n -> p b n", p=P)).then_inc(s_xg[n], 16)
            for b in range(3, NB):
                load_weights(b)
                store_outputs(b - 3)
            for b in range(NB - 3, NB):
                store_outputs(b)
            of = out.rearrange("b s d -> (b s) d")
            for t in range(T):
                sp.wait_ge(s_fin, 2 * (t + 1))
                sp.dma_start(of[P * t:P * t + ROWS[t], :], acc[0:ROWS[t], t, :]).then_inc(s_out, 16)
            sp.wait_ge(s_out, 16 * T)

        @block.gpsimd
        def _(pool):

            def fill(dst, value):
                pool.memset(dst, value).then_inc(s_set, 1)

            fill(zero[:, :], 0.0)
            fill(bb[0:1, :], 0.0)
            fill(xT[:, :, :], 1.0)
            fill(mT[:, :, :], 1.0)
            fill(mvz[:, :, :], 0.0)
            fill(q[:, :, N:N + 64], 0.0)
            fill(xrf[:, 2 * XR:2 * XR + P], 0.0)
            fill(Eb[:, :, 4 * M:], 0.0)
            fill(mv[:, :, :], 1.0)
            fill(pT[:, :, :, 0:1], 0.0)
            fill(bk[:, :], 1.0)
            pool.dma_start(mf[:, :], memory[0]).then_inc(s_mem, 16)
            pool.dma_start(wm[0:H, :, :], w_mem.rearrange("(a p) n -> p a n", p=H)).then_inc(s_mem, 16)
            pool.wait_ge(s_wz, 1)
            pool.dma_start(wm[H:H + 1, 1, :], b_mem.rearrange("(a n) -> a n", a=1)).then_inc(s_mem, 16)
            pool.dma_start(pc[0:1, :], cls_tok[0]).then_inc(s_pos, 16)
            pool.dma_start(pc[1:S, :], pos_emb).then_inc(s_pos, 16)
            pool.dma_start(bb[1:S, :], tok_b.rearrange("(a n) -> a n", a=1).broadcast_to([NP_, D])).then_inc(s_pos, 16)
            fill(eps[:, :], 1e-5)
            fill(half[:, :], -0.5)
            fill(aT[:, :, :], 1.0)
            fill(a1T[:, :, :], 1.0)
            fill(fT[:, :, :], 1.0)
            fill(lg[:, :, :], 0.0)
            fill(m8[:, :, :], 0.0)
            fill(i8[:, :, :], 0)
            fill(one32[:, :], 1.0)
            fill(feats[:, :], 1.0)
            fill(oneb[:, :], 1.0)
            fill(ohs[:, :, :], 0.0)
            fill(XT[:, :, :, :], 1.0)
            pool.wait_ge(s_set, 24)
            pool.dma_start(xs_dram.rearrange("(b p) n -> p b n", p=P), zero[:, None, :].broadcast_to([P, NB, D])).then_inc(s_zs, 16)
            pool.wait_ge(s_cst, 16)
            pool.tensor_copy(sel[:, :, :], ident[0:S, None, 0:S].broadcast_to([S, B, S])).then_inc(s_sel, 1)
            pool.wait_ge(s_pos, 48)
            pool.tensor_tensor(pc[:, :], pc[:, :], bb[:, :], ALU.add).then_inc(s_pc, 1)

            def rstd_of(n):
                pool.wait_ge(s_ag, T * (n + 1))
                pool.tensor_tensor(rstd[:, :], mv[:, :, 1], eps[:, :], ALU.add).then_inc(s_ve, 1)
                pool.wait_ge(s_ve, n + 1)
                pool.tensor_tensor(rstd[:, :], rstd[:, :], half[:, :], ALU.pow).then_inc(s_rstd, 1)

            rstd_of(0)
            pool.wait_ge(s_rstd, 1)
            pool.memset(W1[H:P, :, :, :], 0.0).then_inc(s_w1z, 1)
            pool.wait_ge(s_w1z, 1)
            for i in range(NU):
                m, nh, w = unit_shape(i)
                pool.wait_ge(s_ri, i + 1)
                e = unit_tile(Eb[:, i % NE_, :], i)
                pool.tensor_tensor(e, e, rs[0:m, i % NE_, 0:nh, None].broadcast_to([m, nh, w]), ALU.mult).then_inc(s_pr, 1)
            rstd_of(1)
            pool.wait_ge(s_vrc, 2)
            for r, v in enumerate((vrow, vrev)):
                pool.dma_start(ar[B * r:B * r + B, :], v[:, :].rearrange("p (b s) -> p b s", b=B)).then_inc(s_ar, 16)
            pool.wait_ge(s_zs, 16)
            pool.wait_ge(s_sl, 1)
            for t in range(T):
                for k in range(2):
                    pool.indirect_dma_start(out=xs_dram, out_offset=bass.IndirectOffsetOnAxis(ap=sli[0:ROWS[t], k, t:t + 1], axis=0),
                                            in_=xn[0:ROWS[t], t, :], in_offset=None).then_inc(s_sct, 16)
            pool.wait_ge(s_sn, 1)
            pool.dma_start(bw[:, :, :], dre[B:2 * B, :, :]).then_inc(s_bwd, 16)
            pool.wait_ge(s_z, 1)
            for r in range(2):
                pool.dma_start(feats[E + r:E + r + 1, :].rearrange("p (b s) -> p b s", b=B), ft[:, r, :]).then_inc(s_fe, 16)
            for i in range(3):
                pool.wait_ge(s_yo[i], 16 * len(range(i, NB, 3)))
            for t in range(T):
                for k in range(2):
                    n = 2 * t + k
                    pool.indirect_dma_start(out=yg[0:ROWS[t], k, t, :], out_offset=None, in_=ys_dram,
                                            in_offset=bass.IndirectOffsetOnAxis(ap=sli[0:ROWS[t], k, t:t + 1], axis=0)).then_inc(s_gg[k], 16)

        @block.scalar
        def _(act):
            act.wait_ge(s_mt, 1)
            act.wait_ge(s_set, 4)
            act.activation(mT[0:H, :, :], ps[0:H, 6, 0:256].rearrange("p (a m) -> p a m", a=2)[:, :, 0:M], ACT.Copy).then_inc(s_mtc, 1)
            act.wait_ge(s_mkv, 1)
            act.wait_ge(s_cst, 16)
            for j in range(HH):
                act.activation(mkd[:, :, j, :], ps[:, 7, 0:256].rearrange("p (a m) -> p a m", a=2)[:, :, 0:M], ACT.Copy,
                               scale=headmask[:, j:j + 1]).then_inc(s_mkc, 1)
            for n in range(1, 2 * CK, 2):
                act.wait_ge(s_pt, n + 1)
                c, g = n // 2, n % 2
                act.activation(pT[:, c, :, 1:S].rearrange("p b (gh gw) -> p gw b gh", gw=GRID)[:, 3 * g:3 * g + 3],
                               ps[:, n % 4, 0:3 * B * GRID].rearrange("p (gw b gh) -> p gw b gh", gw=3, b=B),
                               ACT.Copy).then_inc(s_ptc_a, 1)
            act.wait_ge(s_xt, T)
            act.wait_ge(s_set, 3)
            act.activation(xT[0:H, 1, :], psf[0:H, 1024:1024 + N], ACT.Copy).then_inc(s_xtc, 1)

            def halves_of(dst):
                return dst.rearrange("p (a n) -> p a n", a=2)

            act.wait_ge(s_k, 1)
            for j in range(HH):
                act.activation(halves_of(kd[:, 0, j, :]), ps[:, 0:2, 0:N2], ACT.Copy, scale=headmask[:, j:j + 1]).then_inc(s_kc_a, 1)
            for m in range(2):
                act.wait_ge(s_q, m + 1)
                act.activation(halves_of(q[:, m, 0:N]), ps[:, 4 + 2 * m:6 + 2 * m, 0:N2], ACT.Copy).then_inc(s_qc, 1)

            def exps(i):
                act.wait_ge(s_sub, i + 1)
                e = unit_tile(Eb[:, i % NE_, :], i)
                act.activation(e, e, ACT.Exp).then_inc(s_exp, 1)

            def copy_probs(i):
                kind, a, g = UNITS[i]
                for r in range(2 if kind == "self" else 1):
                    k = PT0[i] + r
                    act.wait_ge(s_tp, k + 1)
                    if k >= NPT:
                        act.wait_ge(s_o, max(j for j in range(NU) if PT0[j] <= k - NPT) + 1)
                    if kind == "self":
                        act.activation(PTs[:, k % NPT, 0:3 * P], ps[:, PT_BANK[k % 3], 0:3 * P], ACT.Copy).then_inc(s_tpc, 1)
                    else:
                        m = ROWS[a]
                        act.activation(PTs[:, k % NPT, :].rearrange("p (c m) -> p c m", c=4)[:, :, 0:m],
                                       ps[:, PT_BANK[k % 3], :].rearrange("p (c m) -> p c m", c=4)[:, :, 0:m],
                                       ACT.Copy).then_inc(s_tpc, 1)

            for i in range(NU + LAG_PROBS):
                if i < NU:
                    exps(i)
                if i >= LAG_PROBS:
                    copy_probs(i - LAG_PROBS)

            for a in range(2):
                act.wait_ge(s_al, a + 1)
                act.activation(th[:, :, a * N2:(a + 1) * N2], ps[0:H, 2 * a:2 * a + 2, 0:N2], ACT.Tanh, scale=0.5).then_inc(s_th, 1)
            act.wait_ge(s_xt, 2 * T)
            act.activation(xT[0:H, 1, :], psf[0:H, 1024:1024 + N], ACT.Copy).then_inc(s_xtc, 1)
            act.wait_ge(s_g1, 1)
            act.activation(g2[:, :], g1[:, :], ACT.Exp).then_inc(s_g2, 1)
            for b in range(NB):
                act.wait_ge(s_bt, b + 1)
                act.wait_ge(s_set, 24)
                act.activation(XT[0:H, b % 2, :, :], ps[0:H, 6 + b % 2, 0:256].rearrange("p (a m) -> p a m", a=2), ACT.Copy).then_inc(s_btc, 1)
                for n in range(2):
                    if n == 0 and b >= 2:
                        act.wait_ge(s_y, b - 1)
                    act.wait_ge(s_h1, 2 * b + n + 1)
                    act.activation(hT[:, b % 2, 3 * n:3 * n + 3, :], ps[:, 2 * (b % 2) + n, 0:3 * P].rearrange("p (f m) -> p f m", f=3),
                                   ACT.Gelu_apprx_tanh).then_inc(s_ge, 1)

        @block.vector
        def _(dve):
            dve.memset(wsb[H:P, :], 0.0).then_inc(s_wz, 1)
            step = {s_sv: 0, s_lgz: 0}

            def link(ins, s=s_sv):
                step[s] += 1
                ins.then_inc(s, 1)
                dve.wait_ge(s, step[s])

            dve.wait_ge(s_mkv, 2)
            dve.wait_ge(s_set, 5)
            mvv = ps[0:M, 5, 0:D].rearrange("p (j a d) -> p j a d", a=2, d=DH)
            for a in range(2):
                dve.tensor_copy(mvz[0:M, a::2, DH * a:DH * a + DH], mvv[:, :, a, :]).then_inc(s_mvc, 1)
            for ih in range(IH):
                dve.wait_ge(s_x[ih], 16)
                dve.tensor_copy(xp[:, :, 8 * ih:8 * ih + 8, :], xs[:, 8 * ih:8 * ih + 8, :].rearrange("p i (g j) -> p g i j", g=GW)).then_inc(s_xp, 1)
            dve.wait_ge(s_set, 10)
            for n in range(0, 2 * CK, 2):
                dve.wait_ge(s_pt, n + 1)
                c, g = n // 2, n % 2
                dve.tensor_copy(pT[:, c, :, 1:S].rearrange("p b (gh gw) -> p gw b gh", gw=GRID)[:, 3 * g:3 * g + 3],
                                ps[:, n % 4, 0:3 * B * GRID].rearrange("p (gw b gh) -> p gw b gh", gw=3, b=B)).then_inc(s_ptc_v, 1)

            def moments(n, t):
                m = ROWS[t]
                dve.wait_ge(s_h, T * n + t + 1)
                dve.bn_stats(st6[0:m, t, :], h[0:m, t, :]).then_inc(s_st, 1)
                dve.wait_ge(s_st, T * n + t + 1)
                dve.bn_aggr(mv[0:m, t, :], st6[0:m, t, :]).then_inc(s_ag, 1)

            def normalise(n):
                dve.wait_ge(s_rstd, n + 1)
                for t in range(T):
                    m = ROWS[t]
                    if n == 1 and t == 0:
                        dve.wait_ge(s_xt, T)
                    dve.tensor_scalar(xn[0:m, t, :], h[0:m, t, :], mv[0:m, t, 0:1], rstd[0:m, t:t + 1], ALU.subtract, ALU.mult).then_inc(s_xn, 1)
                dve.wait_ge(s_xt, T * (n + 1))
                dve.tensor_copy(xT[0:H, 0, :], psf[0:H, 0:N]).then_inc(s_xtc, 1)

            dve.wait_ge(s_set, 9)
            for t in range(T):
                m = ROWS[t]
                dve.wait_ge(s_tok, t + 1)
                dve.tensor_copy(h[0:m, t, :], ps[0:m, 4 + t % 4, 0:D]).then_inc(s_h, 1)
                moments(0, t)
            normalise(0)
            dve.wait_ge(s_xtc, 2)
            for m in range(2):
                dve.tensor_copy(xr[:, m, :, :, :], xT[:, m, :].rearrange("p (b s) -> p b s", b=B)[:, :, None, :].broadcast_to([P, B, 2, S])).then_inc(s_xr, 1)
            dve.wait_ge(s_k, 2)
            for j in range(HH):
                dve.tensor_scalar(kd[:, 1, j, :].rearrange("p (a n) -> p a n", a=2), ps[:, 2:4, 0:N2], headmask[:, j:j + 1], None, ALU.mult).then_inc(s_kc_v, 1)

            def shift(i):
                m, nh, w = unit_shape(i)
                s = unit_tile(ps[:, S_BANK[i % 2], :], i)
                dve.wait_ge(s_sc, i + 1)
                dve.tensor_reduce(mx[0:m, i % NE_, 0:nh], s, AX_X, ALU.max).then_inc(s_mx, 1)
                if i >= NE_:
                    dve.wait_ge(s_tp, PT0[i - NE_ + 1])
                dve.wait_ge(s_mx, i + 1)
                dve.tensor_tensor(unit_tile(Eb[:, i % NE_, :], i), s, mx[0:m, i % NE_, 0:nh, None].broadcast_to([m, nh, w]), ALU.subtract).then_inc(s_sub, 1)

            def sums(i):
                m, nh, w = unit_shape(i)
                dve.wait_ge(s_exp, i + 1)
                dve.tensor_reduce(sm[0:m, i % NE_, 0:nh], unit_tile(Eb[:, i % NE_, :], i), AX_X, ALU.add).then_inc(s_sum, 1)
                dve.wait_ge(s_sum, i + 1)
                dve.reciprocal(rs[0:m, i % NE_, 0:nh], sm[0:m, i % NE_, 0:nh]).then_inc(s_ri, 1)

            def mask_values(i):
                u = UNITS[i][1]
                dve.wait_ge(s_v, u + 1)
                if u >= 2:
                    dve.wait_ge(s_o, SELF[u - 2] + 1)
                dve.tensor_tensor(vbd[:, u % 2, :, :], ps[:, V_BANK, 0:2 * D].rearrange("p (a n) -> p a n", a=2),
                                  vmask[:, None, :].broadcast_to([P, 2, D]), ALU.mult).then_inc(s_vc, 1)

            def copy_heads(i):
                kind, a, g = UNITS[i]
                o = ps[0:H, O_BANK[kind], 0:256].rearrange("p (a m) -> p a m", a=2)
                if kind == "self":
                    w = 2 * S
                    dve.wait_ge(s_o, i + 1)
                    dve.tensor_copy(aT[0:H, :, w * a:w * a + w], o[:, :, 0:w]).then_inc(s_oc[kind], 1)
                elif g == 2:
                    m = ROWS[a]
                    dve.wait_ge(s_o, i + 1)
                    dve.tensor_copy(a1T[0:H, :, P * a:P * a + m], o[:, :, 0:m]).then_inc(s_oc[kind], 1)

            dve.wait_ge(s_set, 15)
            for i in range(NU + LAG_HEADS + 1):
                if i < NU:
                    shift(i)
                    if UNITS[i][0] == "self":
                        mask_values(i)
                if 1 <= i <= NU:
                    sums(i - 1)
                if i > LAG_HEADS:
                    copy_heads(i - LAG_HEADS - 1)

            dve.wait_ge(s_set, 16)
            dve.wait_ge(s_oc["self"], U)
            dve.wait_ge(s_oc["mem"], T)
            dve.wait_ge(s_al, 2)
            dve.tensor_tensor(fT[0:H, :, :], aT[0:H, :, :], a1T[0:H, :, :], ALU.add).then_inc(s_df, 1)
            dve.tensor_tensor(aT[0:H, :, :], aT[0:H, :, :], a1T[0:H, :, :], ALU.subtract).then_inc(s_df, 1)
            dve.wait_ge(s_df, 2)
            for a in range(2):
                n = slice(a * N2, (a + 1) * N2)
                dve.wait_ge(s_th, a + 1)
                dve.scalar_tensor_tensor(out=th[:, :, n], in0=th[:, :, n], scalar=0.5, in1=aT[0:H, :, n], op0=ALU.mult, op1=ALU.mult).then_inc(s_fu, 1)
                dve.wait_ge(s_fu, a + 1)
                dve.scalar_tensor_tensor(out=fT[0:H, :, n], in0=fT[0:H, :, n], scalar=0.5, in1=th[:, :, n], op0=ALU.mult, op1=ALU.add).then_inc(s_ft, 1)
            for t in range(T):
                m = ROWS[t]
                dve.wait_ge(s_pj, t + 1)
                dve.tensor_tensor(h[0:m, t, :], ps[0:m, 4 + t % 4, 0:D], h[0:m, t, :], ALU.add).then_inc(s_h, 1)
                moments(1, t)
            normalise(1)
            dve.wait_ge(s_vr, 1)
            dve.tensor_scalar(vrow[:, :].rearrange("p (a n) -> p a n", a=2), ps[0:1, 4:6, 0:N2], -3.0, 3.0, ALU.max, ALU.min).then_inc(s_vrc, 1)
            dve.wait_ge(s_vrc, 1)
            dve.tensor_copy(vrev[:, :].rearrange("p (b s) -> p b s", b=B), vrow[:, :].rearrange("p (b s) -> p b s", b=B)[:, :, ::-1]).then_inc(s_vrc, 1)
            dve.wait_ge(s_set, 19)
            dve.wait_ge(s_gt, 1)
            for t in range(T):
                m = ROWS[t]
                dve.tensor_copy(lg[0:m, t, :], ps[0:m, 6, 8 * t:8 * t + 8]).then_inc(s_lg, 1)
            for t in range(T):
                dve.wait_ge(s_lg, t + 1)
                dve.max(m8[:, t, :], lg[:, t, :]).then_inc(s_tk, 1)
                dve.wait_ge(s_tk, 2 * t + 1)
                dve.max_index(i8[:, t, :], m8[:, t, :], lg[:, t, :]).then_inc(s_tk, 1)
            dve.wait_ge(s_tk, 2 * T)
            dve.tensor_tensor(g1[:, :], m8[:, :, 1], m8[:, :, 0], ALU.subtract).then_inc(s_g1, 1)
            link(dve.tensor_tensor(i8f[:, :, :], i8[:, :, 0:2], const("no_token")[:, :, None].broadcast_to([P, T, 2]), ALU.add), s_lgz)
            io = const("iota")[:, None, :].broadcast_to([P, T, E])
            dve.tensor_copy(trib[:, :], const("before")).then_inc(s_lgz, 1)
            for k in range(2):
                dve.tensor_tensor(oh[:, k, :, :], i8f[:, :, k:k + 1].broadcast_to([P, T, E]), io, ALU.is_equal).then_inc(s_lgz, 1)
            dve.wait_ge(s_lgz, 4)
            dve.wait_ge(s_set, 23)
            dve.tensor_tensor(ohs[:, 0:T, :], oh[:, 0, :, :], oh[:, 1, :, :], ALU.add).then_inc(s_lgz, 1)
            dve.wait_ge(s_rt, 1)
            rank = ps[:, 7, 0:(T + 1) * E].rearrange("p (t e) -> p t e", e=E)
            steps = [5]

            def route(ins):
                steps[0] += 1
                ins.then_inc(s_lgz, 1)
                dve.wait_ge(s_lgz, steps[0])

            route(dve.tensor_tensor(cmp5[:, :, :], rank[:, T, :, None].broadcast_to([P, E, T]), const("blocks_from")[:, None, :].broadcast_to([P, E, T]), ALU.is_gt))
            route(dve.tensor_reduce(nblk[:, :], cmp5[:, :, :], AX_X, ALU.add))
            route(dve.tensor_tensor(cmp8[:, :, :], nblk[:, None, :].broadcast_to([P, E, E]), const("earlier").rearrange("p (a e) -> p a e", a=E), ALU.mult))
            route(dve.tensor_reduce(base[:, :], cmp8[:, :, :], AX_X, ALU.add))
            route(dve.tensor_tensor(cend[:, :], base[:, :], nblk[:, :], ALU.add))
            route(dve.tensor_tensor(cmpb[:, :, :], const("block", 1)[:, :, None].broadcast_to([1, NB, E]), cend[0:1, None, :].broadcast_to([1, NB, E]), ALU.is_ge))
            route(dve.tensor_reduce(ebf[:, :], cmpb[:, :, :], AX_X, ALU.add))
            dve.tensor_scalar(ebi[:, :], ebf[:, :], float(E - 1), None, ALU.min).then_inc(s_eb, 1)
            route(dve.tensor_scalar(base[:, :], base[:, :], float(P), None, ALU.mult))
            route(dve.tensor_tensor(rb[:, :, :], rank[:, 0:T, :], base[:, None, :].broadcast_to([P, T, E]), ALU.add))
            route(dve.tensor_tensor(sl3[:, :, :, :].rearrange("p k t e -> p k (t e)"), oh[:, :, :, :].rearrange("p k t e -> p k (t e)"),
                                    rb[:, :, :].rearrange("p t e -> p (t e)")[:, None, :].broadcast_to([P, 2, T * E]), ALU.mult))
            route(dve.tensor_reduce(slf[:, :, :], sl3[:, :, :, :], AX_X, ALU.add))
            dve.tensor_copy(sli[:, :, :], slf[:, :, :]).then_inc(s_sl, 1)
            dve.wait_ge(s_g2, 1)
            route(dve.tensor_scalar(c1[:, :], g2[:, :], 1.0, None, ALU.add))
            route(dve.reciprocal(c0[:, :], c1[:, :]))
            route(dve.tensor_tensor(c1[:, :], g2[:, :], c0[:, :], ALU.mult))
            for k, c in enumerate((c0, c1)):
                route(dve.tensor_tensor(comb[:, k, :, :], oh[:, k, :, :], c[:, :, None].broadcast_to([P, T, E]), ALU.mult))
            dve.tensor_tensor(comb[:, 0, :, :], comb[:, 0, :, :], comb[:, 1, :, :], ALU.add).then_inc(s_cb, 1)

            def copy_block(b):
                dve.wait_ge(s_y, b + 1)
                if b >= 3:
                    dve.wait_ge(s_yo[b % 3], 16 * (b // 3))
                dve.tensor_copy(ysb[:, b % 3, :], ps[:, 4 + b % 2, 0:D]).then_inc(s_yc, 1)

            dve.wait_ge(s_ct, 1)
            dve.wait_ge(s_set, 21)
            dve.tensor_copy(feats[0:E, :], psf[0:E, 6 * 512:6 * 512 + N]).then_inc(s_ctc, 1)
            dve.wait_ge(s_ar, 32)
            link(dve.tensor_scalar(ar[:, :], ar[:, :], -2.0, None, ALU.add))
            link(dve.tensor_tensor(asg[:, :], ar[:, :], const("alternate", 2 * B), ALU.mult))
            dve.tensor_copy(dre[:, 0, 1:2], one32[:, :])
            link(dve.tensor_copy(dre[:, 0, 0:1], asg[:, 0:1]))
            for n in range(1, S):
                if n % 4 == 3:
                    copy_block(n // 4)
                link(dve.tensor_tensor(dsq[:, :], dre[:, n - 1, :], dre[:, n - 1, :], ALU.mult))
                link(dve.tensor_reduce(dn[:, :], dsq[:, :], AX_X, ALU.add))
                link(dve.reciprocal(dri[:, :], dn[:, :]))
                dve.tensor_scalar(dre[:, n, 0:1], dre[:, n - 1, 0:1], dri[:, 0:1], asg[:, n:n + 1], ALU.mult, ALU.add)
                link(dve.tensor_scalar(dre[:, n, 1:2], dre[:, n - 1, 1:2], dri[:, 0:1], 1.0, ALU.mult, ALU.add))
            dve.tensor_tensor(dre[:, :, 0], dre[:, :, 0], const("alternate", 2 * B), ALU.mult).then_inc(s_sn, 1)
            dve.wait_ge(s_bwd, 16)
            rev = bw[:, ::-1, :]
            link(dve.tensor_tensor(z[:, :, :], dre[0:B, :, :], rev, ALU.add))
            link(dve.tensor_tensor(z[:, :, 0], z[:, :, 0], ar[0:B, :], ALU.subtract))
            link(dve.tensor_scalar(z[:, :, 1], z[:, :, 1], -1.0, None, ALU.add))
            link(dve.tensor_tensor(zz[:, :, :], z[:, :, :], z[:, :, :], ALU.mult))
            link(dve.tensor_reduce(zn[:, :], zz[:, :, :], AX_X, ALU.add))
            link(dve.reciprocal(zr[:, :], zn[:, :]))
            link(dve.tensor_tensor(ft[:, :, :], z[:, :, :].rearrange("p s c -> p c s"), zr[:, None, :].broadcast_to([B, 2, S]), ALU.mult))
            dve.tensor_scalar(ft[:, :, :], ft[:, :, :], -10.0, 10.0, ALU.max, ALU.min).then_inc(s_z, 1)
            dve.wait_ge(s_ow, 64)
            dve.tensor_tensor(ow[:, :], ow[:, :], bk[:, :], ALU.mult).then_inc(s_owb, 1)
            for b in range(9, NB):
                if b == 12:
                    for t in range(T):
                        m = ROWS[t]
                        dve.wait_ge(s_sp, t + 1)
                        dve.tensor_tensor(acc[0:m, t, :], ps[0:m, 6 + t % 2, 256:256 + D], h[0:m, t, :], ALU.add).then_inc(s_ba, 1)
                copy_block(b)
            for t in range(T):
                m = ROWS[t]
                for k, c in enumerate((c0, c1)):
                    dve.wait_ge(s_gg[k], 16 * T)
                    dve.wait_ge(s_ba if k == 0 else s_fin, T if k == 0 else 2 * t + 1)
                    dve.scalar_tensor_tensor(out=acc[0:m, t, :], in0=yg[0:m, k, t, :], scalar=c[0:m, t:t + 1], in1=acc[0:m, t, :],
                                             op0=ALU.mult, op1=ALU.add).then_inc(s_fin, 1)

        @block.tensor
        def _(pe):
            pe.wait_ge(s_cst, 16)
            pe.wait_ge(s_mem, 48)
            for m in range(2):
                ins = pe.transpose(ps[0:H, 6, 128 * m:128 * m + M], mf[:, H * m:H * m + H], ident[0:M, 0:M])
            ins.then_inc(s_mt, 1)
            pe.wait_ge(s_mtc, 1)
            for m in range(2):
                o = ps[:, 7, 128 * m:128 * m + M]
                pe.matmul(o, wm[:, 0, H * m:H * m + P], mT[:, 0, :], start=True, stop=False)
                ins = pe.matmul(o, wm[:, 1, H * m:H * m + P], mT[:, 1, :], start=False, stop=True)
            ins.then_inc(s_mkv, 1)
            pe.matmul(ps[0:M, 5, 0:D], mT[:, 0, :], wm[:, 0, D:2 * D], start=True, stop=False)
            pe.matmul(ps[0:M, 5, 0:D], mT[:, 1, :], wm[:, 1, D:2 * D], start=False, stop=True).then_inc(s_mkv, 1)
            for n in range(2 * CK):
                c, g = n // 2, n % 2
                if n >= 4:
                    if n % 2:
                        pe.wait_ge(s_ptc_a, (n - 4) // 2 + 1)
                    else:
                        pe.wait_ge(s_ptc_v, (n - 4) // 2 + 1)
                pe.wait_ge(s_xp, c // (CK // IH) + 1)
                for a in range(3):
                    patch = xp[:, 3 * g + a, :, :].rearrange("p i j -> p (i j)")
                    ins = pe.transpose(ps[:, n % 4, a * 96:a * 96 + 96], patch[:, P * c:P * c + P], ident[0:96, 0:96])
                ins.then_inc(s_pt, 1)
            pe.wait_ge(s_sel, 1)
            pe.wait_ge(s_pc, 1)
            pe.wait_ge(s_wt, 16)
            pe.wait_ge(s_mvc, 2)
            pe.wait_ge(s_mkc, HH)
            pe.wait_ge(s_ptc_a, CK)
            pe.wait_ge(s_ptc_v, CK)
            self_ = sel[:, :, :].rearrange("p b s -> p (b s)")
            for t in range(T):
                m = ROWS[t]
                if t >= 4:
                    pe.wait_ge(s_h, t - 3)
                o = ps[0:m, 4 + t % 4, 0:D]
                pe.matmul(o, self_[:, P * t:P * t + m], pc[:, :], start=True, stop=False)
                for c in range(CK):
                    ins = pe.matmul(o, pT[:, c, :, :].rearrange("p b s -> p (b s)")[:, P * t:P * t + m], wt[:, c, :],
                                    start=False, stop=(c == CK - 1))
                ins.then_inc(s_tok, 1)

            def to_features(n):
                for t in range(T):
                    m = ROWS[t]
                    pe.wait_ge(s_xn, T * n + t + 1)
                    pe.transpose(psf[0:H, P * t:P * t + m], xn[0:m, t, 0:H], ident[0:m, 0:m])
                    pe.transpose(psf[0:H, 1024 + P * t:1024 + P * t + m], xn[0:m, t, H:D], ident[0:m, 0:m]).then_inc(s_xt, 1)

            to_features(0)
            pe.wait_ge(s_xtc, 2)
            pe.wait_ge(s_wat, 32)

            def project(col, b0):
                for a in range(2):
                    n = slice(a * N2, (a + 1) * N2)
                    o = ps[:, b0 + a, 0:N2]
                    pe.matmul(o, wa[:, 0, col:col + P], xT[:, 0, n], start=True, stop=False)
                    ins = pe.matmul(o, wa[:, 1, col:col + P], xT[:, 1, n], start=False, stop=True)
                return ins

            project(D, 0).then_inc(s_k, 1)
            project(D + H, 2).then_inc(s_k, 1)
            project(0, 4).then_inc(s_q, 1)
            project(H, 6).then_inc(s_q, 1)
            pe.wait_ge(s_qc, 2)
            pe.wait_ge(s_kc_a, HH)
            pe.wait_ge(s_kc_v, HH)
            pe.wait_ge(s_xr, 2)

            def scores(i):
                kind, a, g = UNITS[i]
                s = ps[:, S_BANK[i % 2], :]
                if i >= 2:
                    pe.wait_ge(s_sub, i - 1)
                if kind == "self":
                    for r in range(2):
                        n0 = (2 * a + r) * S
                        for m in range(2):
                            ins = pe.matmul(s[64 * r:64 * r + 64, HH * S * m:HH * S * (m + 1)], q[:, m, n0:n0 + 64],
                                            kd[:, m, :, n0:n0 + S], start=True, stop=True)
                else:
                    rows = ROWS[a]
                    for m, h0, h1, c0_ in (((0, 0, 4, 0),), ((0, 4, 6, 0), (1, 0, 2, 2 * M)), ((1, 2, 6, 0),))[g]:
                        ins = pe.matmul(s[0:rows, c0_:c0_ + (h1 - h0) * M], q[:, m, P * a:P * a + rows], mkd[:, m, h0:h1, :],
                                        start=True, stop=True)
                ins.then_inc(s_sc, 1)

            def values(i):
                u = UNITS[i][1]
                if u >= 1:
                    pe.wait_ge(s_vc, u)
                for r in range(2):
                    o = ps[:, V_BANK, D * r:D * (r + 1)]
                    c = (2 * u + r) * 2 * S
                    pe.matmul(o, xrf[:, c:c + P], wa[:, 0, 2 * D:3 * D], start=True, stop=False)
                    ins = pe.matmul(o, xrf[:, XR + c:XR + c + P], wa[:, 1, 2 * D:3 * D], start=False, stop=True)
                ins.then_inc(s_v, 1)

            def transposes(i):
                kind, a, g = UNITS[i]
                e = Eb[:, i % NE_, :]
                pe.wait_ge(s_pr, i + 1)
                for r in range(2 if kind == "self" else 1):
                    k = PT0[i] + r
                    if k >= 3:
                        pe.wait_ge(s_tpc, k - 2)
                    o = ps[:, PT_BANK[k % 3], :]
                    if kind == "self":
                        for c in range(3):
                            h0 = 2 * (3 * r + c) * S
                            ins = pe.transpose(o[:, P * c:P * c + P], e[:, h0:h0 + P], ident)
                    else:
                        m = ROWS[a]
                        for c in range(4):
                            ins = pe.transpose(o[:, P * c:P * c + m], e[0:m, c * M:c * M + P], ident[0:m, 0:m])
                    ins.then_inc(s_tp, 1)

            def heads(i):
                kind, a, g = UNITS[i]
                o = ps[:, O_BANK[kind], :]
                if a and not g:
                    pe.wait_ge(s_oc[kind], a)
                if kind == "self":
                    pe.wait_ge(s_tpc, PT0[i] + 2)
                    pe.wait_ge(s_vc, a + 1)
                    for c in range(6):
                        pt = PTs[:, (PT0[i] + c // 3) % NPT, P * (c % 3):P * (c % 3) + P]
                        for r in range(2):
                            c0_ = (c // 3) * P + r * S
                            ins = pe.matmul(o[32 * (c % 3):32 * (c % 3) + 32, c0_:c0_ + S], vbd[:, a % 2, r, 32 * c:32 * c + 32],
                                            pt[:, 64 * r:64 * r + S], start=True, stop=True)
                else:
                    pe.wait_ge(s_tpc, PT0[i] + 1)
                    m = ROWS[a]
                    pt = PTs[:, PT0[i] % NPT, :]
                    for c in range(4):
                        j = 2 * g + c // 2
                        ins = pe.matmul(o[32 * (j % 3):32 * (j % 3) + 32, (j // 3) * P:(j // 3) * P + m], mvz[:, 4 * g + c, :],
                                        pt[:, P * c:P * c + m], start=(c % 2 == 0), stop=(c % 2 == 1))
                ins.then_inc(s_o, 1)

            for i in range(NU + LAG_HEADS):
                if i < NU:
                    scores(i)
                    if UNITS[i][0] == "self":
                        values(i)
                if LAG_PROBS <= i < NU + LAG_PROBS:
                    transposes(i - LAG_PROBS)
                if i >= LAG_HEADS:
                    heads(i - LAG_HEADS)

            pe.wait_ge(s_wal, 64)
            pe.wait_ge(s_oc["self"], U)
            pe.wait_ge(s_oc["mem"], T)
            for a in range(2):
                n = slice(a * N2, (a + 1) * N2)
                for m in range(2):
                    o = ps[0:H, 2 * a + m, 0:N2]
                    c = slice(H * m, H * m + H)
                    pe.matmul(o, wal[:, 0, c], aT[:, 0, n], start=True, stop=False)
                    pe.matmul(o, wal[:, 1, c], aT[:, 1, n], start=False, stop=False)
                    pe.matmul(o, wal[:, 2, c], a1T[:, 0, n], start=False, stop=False)
                    ins = pe.matmul(o, wal[:, 3, c], a1T[:, 1, n], start=False, stop=True)
                ins.then_inc(s_al, 1)
            for t in range(T):
                m = ROWS[t]
                n = slice(P * t, P * t + m)
                pe.wait_ge(s_ft, 1 if P * t + m <= N2 else 2)
                if t >= 4:
                    pe.wait_ge(s_h, T + t - 3)
                o = ps[0:m, 4 + t % 4, 0:D]
                pe.matmul(o, fT[:, 0, n], wp[:, 0, :], start=True, stop=False)
                pe.matmul(o, fT[:, 1, n], wp[:, 1, :], start=False, stop=True).then_inc(s_pj, 1)
            to_features(1)
            pe.wait_ge(s_gw, 80)
            pe.wait_ge(s_xtc, 4)
            for t in range(T):
                m = ROWS[t]
                n = slice(P * t, P * t + m)
                pe.matmul(ps[0:m, 6, 8 * t:8 * t + 8], xT[:, 0, n], gv[:, 0, :], start=True, stop=False)
                ins = pe.matmul(ps[0:m, 6, 8 * t:8 * t + 8], xT[:, 1, n], gv[:, 1, :], start=False, stop=True)
            ins.then_inc(s_gt, 1)
            for a in range(2):
                n = slice(a * N2, (a + 1) * N2)
                pe.matmul(ps[0:1, 4 + a, 0:N2], vw[:, 0, :], xT[:, 0, n], start=True, stop=False)
                ins = pe.matmul(ps[0:1, 4 + a, 0:N2], vw[:, 1, :], xT[:, 1, n], start=False, stop=True)
            ins.then_inc(s_vr, 1)
            pe.wait_ge(s_lgz, 5)
            rank = ps[:, 7, 0:(T + 1) * E]
            pe.matmul(rank, trib[:, :], ohs[:, :, :], start=True, stop=False)
            for t in range(T):
                ins = pe.matmul(rank[:, (t + 1) * E:], oneb[:, :], ohs[:, t:t + 1, :].broadcast_to([P, T - t, E]), start=False, stop=(t == T - 1))
            ins.then_inc(s_rt, 1)
            pe.wait_ge(s_cb, 1)
            for t in range(T):
                m = ROWS[t]
                ins = pe.transpose(psf[0:E, 6 * 512 + P * t:6 * 512 + P * t + m], comb[0:m, 0, t, :], ident[0:m, 0:m])
            ins.then_inc(s_ct, 1)
            pe.wait_ge(s_ctc, 1)

            def spread(b):
                pe.wait_ge(s_xg[0 if b < 2 else 1], 16)
                if b >= 2:
                    pe.wait_ge(s_btc, b - 1)
                for m in range(2):
                    ins = pe.transpose(ps[0:H, 6 + b % 2, P * m:P * m + P], xg[:, b, H * m:H * m + H], ident)
                ins.then_inc(s_bt, 1)

            def hidden(b):
                w = b % NW
                pe.wait_ge(s_w[w], 48 * (b // NW + 1))
                pe.wait_ge(s_btc, b + 1)
                if b >= 2:
                    pe.wait_ge(s_ge, 2 * b - 2)
                for f in range(FM):
                    o = ps[:, 2 * (b % 2) + f // 3, P * (f % 3):P * (f % 3) + P]
                    pe.matmul(o, W1[:, w, 0, P * f:P * f + P], XT[:, b % 2, 0, :], start=True, stop=False)
                    ins = pe.matmul(o, W1[:, w, 1, P * f:P * f + P], XT[:, b % 2, 1, :], start=False, stop=True)
                    if f % 3 == 2:
                        ins.then_inc(s_h1, 1)

            def outputs(b):
                w = b % NW
                if b >= 2:
                    pe.wait_ge(s_yc, b - 1)
                o = ps[:, 4 + b % 2, 0:D]
                for f in range(FM):
                    if f % 3 == 0:
                        pe.wait_ge(s_ge, 2 * b + f // 3 + 1)
                    ins = pe.matmul(o, hT[:, b % 2, f, :], W2[:, w, f, :], start=(f == 0), stop=(f == FM - 1))
                ins.then_inc(s_y, 1)

            spread(0)
            for b in range(NB):
                if b + 1 < NB:
                    spread(b + 1)
                hidden(b)
                if b >= 1:
                    outputs(b - 1)
                if b == 12:
                    pe.wait_ge(s_owb, 1)
                    pe.wait_ge(s_fe, 32)
                    for t in range(T):
                        m = ROWS[t]
                        if t >= 2:
                            pe.wait_ge(s_ba, t - 1)
                        pe.wait_ge(s_btc, 14)
                        pe.matmul(ps[0:m, 6 + t % 2, 256:256 + D], feats[:, P * t:P * t + m], ow[:, :], start=True, stop=True).then_inc(s_sp, 1)
                    pe.wait_ge(s_ba, T)
            outputs(NB - 1)


_INS = ["x", "cls_tok", "L0_tok_W", "L0_tok_b", "L0_tok_pos_emb", "L0_attn_w_attn", "L0_attn_b_attn", "L0_attn_w_proj",
        "L0_attn_b_proj", "L0_attn_w_mem", "L0_attn_b_mem", "L0_attn_w_alpha", "L0_attn_b_alpha", "L0_attn_memory_features",
        "L0_ffn_v_w", "L0_ffn_v_b", "L0_ffn_gate_w", "L0_ffn_gate_b", "L0_ffn_w1", "L0_ffn_b1", "L0_ffn_w2", "L0_ffn_b2",
        "L0_ffn_out_w", "L0_ffn_out_b", "L0_ffn_bk_scale"]


def kernel(**inputs):
    import numpy as _np
    import concourse.bacc as _bacc
    from concourse import mybir as _mybir
    from concourse.bass_utils import run_bass_kernel_spmd as _run

    nc = _bacc.Bacc("TRN2", target_bir_lowering=False, num_devices=1)
    arrays, args = {}, []
    for name in _INS:
        a = _np.ascontiguousarray(inputs[name])
        if a.ndim == 0:
            a = a.reshape(1, 1)
        arrays[f"in_{name}"] = a
        args.append(nc.dram_tensor(f"in_{name}", a.shape, _mybir.dt.from_np(a.dtype), kind="ExternalInput").ap())
    p = _np.arange(128)[:, None]
    e = _np.arange(8)
    tables = {
        "ident": p == _np.arange(128),
        "headmask": p // 16 == _np.arange(6),
        "vmask": p // 37 == (_np.arange(192) // 16) % 2,
        "iota": e + 0 * p,
        "blocks_from": 128 * _np.arange(5) + 0 * p,
        "earlier": (e[None, :] < e[:, None]).reshape(1, 64) + 0 * p,
        "block": _np.arange(17) + 0 * p,
        "no_token": 100 * (128 * _np.arange(5) + p >= 592),
        "before": p < _np.arange(128),
        "alternate": 1 - 2 * (_np.arange(37) % 2) + 0 * p,
    }
    consts = _np.concatenate([tables[name] for name, _ in CONSTS], axis=1).astype(_np.float32)
    arrays["in_consts"] = consts
    args.append(nc.dram_tensor("in_consts", consts.shape, _mybir.dt.float32, kind="ExternalInput").ap())
    args.append(nc.dram_tensor("out_0", (16, 37, 192), _mybir.dt.float32, kind="ExternalOutput").ap())
    vit_block(nc, *args)
    r = _run(nc, [arrays], core_ids=[0])
    return r.results[0]["out_0"]
```

```python
from contextlib import ExitStack

import concourse.bass as bass
from concourse import mybir

ALU = mybir.AluOpType
ACT = mybir.ActivationFunctionType
F32 = mybir.dt.float32
U32 = mybir.dt.uint32
I32 = mybir.dt.int32
BF16 = mybir.dt.bfloat16
AX_X = mybir.AxisListType.X

P = 128


CONSTS = (("ident", 128), ("headmask", 6), ("vmask", 192), ("iota", 8), ("blocks_from", 5), ("through", 64),
          ("block", 17), ("no_token", 5), ("before", 128), ("alternate", 37),
          ("region", 8), ("token", 5), ("dummy", 1))


def vit_block(nc, x, cls_tok, tok_w, tok_b, pos_emb, w_attn, b_attn, w_proj, b_proj, w_mem, b_mem, w_alpha, b_alpha,
              memory, v_w, v_b, gate_w, gate_b, w1, b1, w2, b2, out_w, out_b, bk_scale, consts, out):
    B, IMG, _, CH = x.shape
    PDIM, D = tok_w.shape
    GRID = 6
    PATCH = IMG // GRID
    NP_ = GRID * GRID
    S = NP_ + 1
    N = B * S
    N2 = N // 2
    NH, DH = 12, 16
    M = memory.shape[1]
    E, _, F = w1.shape
    H = D // 2
    HH = NH // 2
    T = -(-N // P)
    ROWS = [min(P, N - P * t) for t in range(T)]
    ROW = CH * PATCH
    IH = 2
    CK = PDIM // P
    GW = GRID
    NB = (2 * N - E) // P + E
    DS = D + 2
    NW = 3
    FM = F // P
    U = B // 2

    with ExitStack() as ctx:
        def sb(name, shape, dt=F32):
            return ctx.enter_context(nc.sbuf_tensor(name, shape, dt))

        def sem(name):
            return ctx.enter_context(nc.semaphore(name))

        ps = ctx.enter_context(nc.psum_tensor("ps", [P, 8, 512], F32))
        psf = ps[:, :, :].rearrange("p a b -> p (a b)")

        at = 0
        named = {}
        for name, width in CONSTS:
            named[name] = (at, at + width)
            at += width
        cst = sb("cst", [P, at])

        def const(name, rows=P):
            return cst[0:rows, named[name][0]:named[name][1]]

        ident = const("ident")
        headmask = const("headmask")
        vmask = const("vmask")

        early = sb("early", [P, 2 * PATCH * IMG * CH])
        xs = early[0:B * GRID, 0:PATCH * IMG * CH].rearrange("p (i j) -> p i j", i=PATCH)
        xp = early[0:B * GRID, PATCH * IMG * CH:].rearrange("p (g i j) -> p g i j", g=GW, i=PATCH)
        wt = sb("wt", [P, CK, D])
        pT = sb("pT", [P, CK, B, S])
        sel = sb("sel", [S, B, S])
        pc = sb("pc", [S, D])
        bb = sb("bb", [S, D])
        h = sb("h", [P, T, D])
        xn = sb("xn", [P, T, D])
        st6 = sb("st6", [P, T, 6])
        mv = sb("mv", [P, T, 2])
        eps = sb("eps", [P, T])
        half = sb("half", [P, T])
        rstd = sb("rstd", [P, T])
        xT = sb("xT", [P, 2, N])
        XR = B * 2 * S
        xrf = sb("xr", [P, 2 * XR + P])
        xr = xrf[:, 0:2 * XR].rearrange("p (m b r s) -> p m b r s", m=2, b=B, r=2)
        wsb = sb("wsb", [P, 16 * D + 2 * E + 2])
        wcol = [0]

        def weights(halves, n):
            c = wcol[0]
            wcol[0] += halves * n
            return wsb[:, c:c + halves * n].rearrange("p (a n) -> p a n", a=halves)

        wm = weights(2, 2 * D)
        wa = weights(2, 3 * D)
        wal = weights(4, D)
        wp = weights(2, D)
        gv = weights(2, E)
        vw = weights(2, 1)
        q = sb("q", [P, 2, N + 64])
        mid = sb("mid", [P, 2 * HH * N])
        kd = mid[:, :].rearrange("p (m j n) -> p m j n", m=2, j=HH)
        xg = mid[:, 0:NB * DS].rearrange("p (b n) -> p b n", b=NB)
        mf = sb("mf", [M, D])
        mT = sb("mT", [P, 2, M])
        mkd = sb("mkd", [P, 2, HH, M])
        mvz = sb("mvz", [P, NH, 32])
        NE_ = 4
        Eb = sb("Eb", [P, NE_, 512])
        mx = sb("mx", [P, NE_, NH])
        sm = sb("sm", [P, NE_, NH])
        rs = sb("rs", [P, NE_, NH])
        NPT = 3
        PTs = sb("PTs", [P, NPT, 512])
        vbd = sb("vbd", [P, 2, 2, D])
        aT = sb("aT", [P, 2, N])
        a1T = sb("a1T", [P, 2, N])
        th = sb("th", [H, 2, 2, P])
        df = sb("df", [H, 2, 2, P])
        fT = sb("fT", [P, 2, N])
        lg = sb("lg", [P, T, E])
        m8 = sb("m8", [P, T, 8])
        i8 = sb("i8", [P, T, 8], U32)
        i8f = sb("i8f", [P, 2])
        g1 = sb("g1", [P, T])
        g2 = sb("g2", [P, T])
        g3 = sb("g3", [P, T])
        oh = sb("oh", [P, 2, T, E])
        ohs = sb("ohs", [P, T, E], BF16)
        trib = sb("trib", [P, P], BF16)
        oneb = sb("oneb", [P, P], BF16)
        cmp5 = sb("cmp5", [P, E, T])
        nblk = sb("nblk", [P, E])
        cmp8 = sb("cmp8", [P, E, E])
        base = sb("base", [P, E])
        cend = sb("cend", [P, E])
        cmpb = sb("cmpb", [1, NB, E])
        ebf = sb("ebf", [1, NB])
        ebi = sb("ebi", [1, NB], I32)
        gapb = sb("gapb", [1, NB, E])
        gap = sb("gap", [1, E])
        row_f = sb("row_f", [1, NB])
        row_i = sb("row_i", [1, NB], I32)
        rb = sb("rb", [P, E])
        sl3 = sb("sl3", [P, 2, E])
        slf = sb("slf", [P, 2])
        sli = sb("sli", [P, T, 2], U32)
        zero = sb("zero", [P, DS])
        comb = sb("comb", [P, 2, T, E])
        vrow = sb("vrow", [1, N])
        vrev = sb("vrev", [1, N])
        ar = sb("ar", [2 * B, S])
        asg = sb("asg", [2 * B, S])
        dre = sb("dre", [2 * B, S, 2])
        dsq = sb("dsq", [2 * B, 2])
        dn = sb("dn", [2 * B, 1])
        dri = sb("dri", [2 * B, 1])
        one32 = sb("one32", [2 * B, 1])
        bw = sb("bw", [B, S, 2])
        z = sb("z", [B, S, 2])
        zz = sb("zz", [B, S, 2])
        zn = sb("zn", [B, S])
        zr = sb("zr", [B, S])
        ft = sb("ft", [B, 2, S])
        R = E + 3
        feats = sb("feats", [R, N])
        ow = sb("ow", [R, D])
        bk = sb("bk", [R, D])
        W1 = early[:, 0:NW * 2 * F].rearrange("p (w a f) -> p w a f", w=NW, a=2)
        W2 = early[:, NW * 2 * F:NW * 2 * F + NW * FM * D].rearrange("p (w m n) -> p w m n", w=NW, m=FM)
        XT = sb("XT", [P, 2, 2, P])
        hT = sb("hT", [P, 2, FM, P])
        ysb = sb("ysb", [P, 3, D])
        acc = sb("acc", [P, T, D])
        xk = pT[:, :, :, :].rearrange("p c b s -> p (c b s)")[:, 0:2 * T * DS].rearrange("p (k t n) -> p k t n", k=2, t=T)
        slot_dummy = sb("slot_dummy", [P, NB])
        slot_row = sb("slot_row", [P, NB], U32)
        xs_dram = nc.dram_tensor("slots_in", [T * E + 1, P, DS], F32).ap()
        xs_rows = xs_dram.rearrange("b p n -> (b p) n")
        sums = nc.dram_tensor("sums", [1 + N + P, D], F32).ap()
        side = nc.dram_tensor("side", [1 + N + P, D], F32).ap()
        SIDE = range(1, 9, 2)

        s_cst = sem("consts_landed")
        s_x = [sem(f"image_rows_landed{i}") for i in range(IH)]
        s_wt = sem("patch_weights_landed")
        s_pos = sem("positions_landed")
        s_mem = sem("memory_landed")
        s_wat = sem("attn_weights_landed")
        s_wal = sem("alpha_weights_landed")
        s_gw = sem("gate_weights_landed")
        s_ow = sem("spec_weights_landed")
        s_set = sem("pool_setup")
        s_wz = sem("weight_rows_cleared")
        s_w1z = sem("expert_weight_rows_cleared")
        s_sel = sem("selector_ready")
        s_pc = sem("positions_ready")
        s_mt = sem("memory_transposed")
        s_mtc = sem("memory_transposed_copied")
        s_mkv = sem("memory_kv_ready")
        s_mkc = sem("memory_keys_spread")
        s_mvc = sem("memory_values_spread")
        s_xp = sem("patch_rows_gathered")
        s_xr_a = sem("tokens_repeated_by_act")
        s_xr_v = sem("tokens_repeated_by_dve")
        s_pt = sem("patches_transposed")
        s_ptc_a = sem("patches_copied_by_act")
        s_ptc_v = sem("patches_copied_by_dve")
        s_tok = sem("tokens_summed")
        s_h = sem("tokens_copied")
        s_st = sem("moments_taken")
        s_ag = sem("mean_and_variance")
        s_ve = sem("variance_plus_eps")
        s_rstd = sem("rstd_ready")
        s_xn = sem("tokens_normalised")
        s_xt = sem("tokens_transposed")
        s_xtc_a = sem("tokens_copied_by_act")
        s_xtc_v = sem("tokens_copied_by_dve")
        s_q = sem("queries_summed")
        s_qc = sem("queries_copied")
        s_k = sem("keys_summed")
        s_kc_a = sem("keys_spread_by_act")
        s_kc_v = sem("keys_spread_by_dve")
        s_v = sem("values_summed")
        s_vc = sem("values_masked")
        s_dbf = sem("dve_bank_filled")
        s_mx = sem("score_maxima")
        s_dbr = sem("dve_bank_read")
        s_exp = sem("exps_ready")
        s_sum = sem("exp_sums")
        s_ri = sem("sum_reciprocals")
        s_pr = sem("probs_ready")
        s_abf = sem("act_bank_filled")
        s_abr = sem("act_bank_read")
        s_o = sem("heads_summed")
        s_oc = {kind: sem(f"heads_copied_{kind}") for kind in ("self", "mem")}
        s_df = sem("differences_ready")
        s_fu = sem("fused_products")
        s_ft = sem("fused_ready")
        s_vr = sem("potentials_summed")
        s_vrc = sem("potentials_clipped")
        s_tk = sem("top2_steps")
        s_g1 = sem("gate_differences")
        s_g2 = sem("gate_exps")
        s_ar = sem("scan_inputs_landed")
        s_sn = sem("scan_steps_pool")
        s_sv = sem("scan_steps_dve")
        s_bwd = sem("backward_landed")
        s_z = sem("green_steps")
        s_fe = sem("features_landed")
        s_owb = sem("spec_weights_scaled")
        s_lgz = sem("route_steps")
        s_eb = sem("block_experts_ready")
        s_sl = sem("slots_ready")
        s_cb = sem("shares_ready")
        s_ct = sem("shares_transposed")
        s_ctc = sem("shares_copied")
        s_zs = sem("slots_cleared")
        s_sct = sem("tokens_scattered")
        s_w1 = [sem(f"hidden_weights_landed{i}") for i in range(NW)]
        s_w2 = [sem(f"output_weights_landed{i}") for i in range(NW)]
        s_xg = [sem(f"block_tokens_landed{i}") for i in range(4)]
        s_oh = sem("one_hots_ready")
        s_brow = sem("block_rows_ready")
        s_bt = sem("block_transposed")
        s_btc = sem("block_transposed_copied")
        s_h1 = sem("hidden_summed")
        s_ge = sem("gelu_ready")
        s_y = sem("block_out_summed")
        s_yc = sem("block_out_copied")
        s_sp = sem("spectral_summed")
        s_ba = sem("residual_ready")
        s_id = sem("token_rows_written")
        s_xk = sem("payloads_ready")
        s_dr = sem("dummy_rows_cleared")
        s_res = sem("residual_written")
        s_row = sem("slot_rows_ready")
        s_add = sem("block_added")
        s_side = sem("block_added_aside")
        s_sld = sem("side_sums_landed")
        s_acc = sem("spectral_added")
        s_out = sem("out_written")

        block = ctx.enter_context(nc.Block())

        UNITS = []
        for u in range(U):
            UNITS.append(("self", u, 0))
            UNITS += [("mem", *divmod(j, 3)) for j in range(2 * u, min(2 * u + 2, 3 * T))]
        NU = len(UNITS)
        PT0 = []
        k = 0
        for kind, _, _ in UNITS:
            PT0.append(k)
            k += 2 if kind == "self" else 1
        SELF = [i for i in range(NU) if UNITS[i][0] == "self"]
        assert sum(1 for kind, _, _ in UNITS if kind == "mem") == 3 * T
        DVE_BANK, ACT_BANK, O_BANK, V_BANK = [0, 1, 5], [2, 3, 4], 6, 7
        O_COL = {"self": 0, "mem": 256}
        LAG_PROBS, LAG_HEADS = 3, 4
        PROBS = [i + LAG_PROBS for i in range(NU)]
        HEADS = [i + LAG_HEADS for i in range(NU)]
        LAST_UNIT = [max(i for i in range(NU) if UNITS[i][:1] + UNITS[i][1:2] == ("mem", t)
                         or i in SELF and 2 * S * UNITS[i][1] < P * t + ROWS[t]) for t in range(T)]
        STAGES = [(1, 3, 2, 1, 2)] * (T - 3) + [(1, 2, 2, 1, 2), (4, 1, 2, 1, 1), (1, 1, 2, 1, 1)]
        BLEND, PROJ, TURN, GATE, RANK = ([HEADS[LAST_UNIT[t]] + sum(STAGES[t][:n + 1]) for t in range(T)] for n in range(5))
        STEPS = RANK[-1] + 3
        dve_use, act_use = {}, {}
        for i in range(STEPS):
            if i < NU:
                dve_use["scores", i] = len(dve_use)
            for j in range(NU):
                if i == PROBS[j]:
                    for r in range(2 if UNITS[j][0] == "self" else 1):
                        act_use["probs", j, r] = len(act_use)
            for t in range(T):
                if i == BLEND[t]:
                    act_use["blend", t] = len(act_use)
                if i == PROJ[t]:
                    dve_use["proj", t] = len(dve_use)
                if i == TURN[t]:
                    act_use["turn", t] = len(act_use)
                if i == GATE[t]:
                    dve_use["gate", t] = len(dve_use)
                if i == RANK[t]:
                    dve_use["rank", t] = len(dve_use)
        PAIRS = [-(-(P * t + ROWS[t]) // (2 * S)) for t in range(T)]

        def last_probs(i):
            return act_use["probs", i, 1 if UNITS[i][0] == "self" else 0]

        GROUPS = ((range(0, 3), slice(0, 3 * P)), (range(3, T), slice(3 * P, N)))
        assert 3 * P >= N2
        QK_BANK = ((4, 5, 6, 7), (1, 3, 0, 2))

        def group_bank(g, m):
            return ps[0:H, g + 2 * m, 0:GROUPS[g][1].stop - GROUPS[g][1].start]

        def token_half(a):
            return slice(a * N2, (a + 1) * N2)

        def repeated(m, a):
            b = slice(a * B // 2, (a + 1) * B // 2)
            return xr[:, m, b, :, :], xT[:, m, :].rearrange("p (b s) -> p b s", b=B)[:, b, None, :].broadcast_to([P, B // 2, 2, S])

        def unit_shape(i):
            kind, a, _ = UNITS[i]
            return (P, NH, S) if kind == "self" else (ROWS[a], 4, M)

        def unit_tile(buf, i):
            m, nh, w = unit_shape(i)
            return buf[0:m, 0:nh * w].rearrange("p (h w) -> p h w", h=nh)

        FILLS = "bb pT mv eps half mT xT mvz q xrf Eb bk one32 lg m8 i8 ohs oneb aT a1T fT XT feats zero".split()

        def filled(name):
            return FILLS.index(name) + 1

        def half_blend(eng, t):
            m = ROWS[t]
            n = slice(P * t, P * t + m)
            eng.wait_ge(s_oc["self"], PAIRS[t])
            eng.wait_ge(s_oc["mem"], t + 1)
            eng.tensor_tensor(df[:, t % 2, :, 0:m], aT[0:H, :, n], a1T[0:H, :, n], ALU.subtract).then_inc(s_df, 1)
            eng.tensor_tensor(fT[0:H, :, n], aT[0:H, :, n], a1T[0:H, :, n], ALU.add).then_inc(s_df, 1)

        def blend(eng, t):
            m = ROWS[t]
            n = slice(P * t, P * t + m)
            eng.wait_ge(s_abr, act_use["blend", t] + 1)
            eng.wait_ge(s_df, 2 * t + 2)
            eng.tensor_tensor(df[:, t % 2, :, 0:m], th[:, t % 2, :, 0:m], df[:, t % 2, :, 0:m], ALU.mult).then_inc(s_fu, 1)
            eng.wait_ge(s_fu, t + 1)
            eng.tensor_tensor(fT[0:H, :, n], fT[0:H, :, n], df[:, t % 2, :, 0:m], ALU.add).then_inc(s_ft, 1)

        @block.sync
        def _(sp):
            xv = x.rearrange("b (g i) j c -> (b g) i (j c)", i=PATCH)
            sp.dma_start(cst[:, :], consts).then_inc(s_cst, 16)
            for ih in range(IH):
                sp.dma_start(xs[:, 8 * ih:8 * ih + 8, :], xv[:, 8 * ih:8 * ih + 8, :]).then_inc(s_x[ih], 16)
            sp.dma_start(wt[:, :, :], tok_w.rearrange("(c p) n -> p c n", p=P)).then_inc(s_wt, 16)

            def halves(dst, src, s):
                sp.dma_start(dst, src.rearrange("(a p) n -> p a n", p=H)).then_inc(s, 16)

            def row(dst, src, s):
                sp.dma_start(dst, src.rearrange("(a n) -> a n", a=1)).then_inc(s, 16)

            halves(wa[0:H, :, :], w_attn, s_wat)
            sp.dma_start(mf[:, :], memory[0]).then_inc(s_mem, 16)
            halves(wm[0:H, :, :], w_mem, s_mem)
            sp.wait_ge(s_wz, 1)
            row(wa[H:H + 1, 1, :], b_attn, s_wat)
            row(wm[H:H + 1, 1, :], b_mem, s_mem)
            halves(wal[0:H, :, :], w_alpha, s_wal)
            row(wal[H:H + 1, 3, :], b_alpha, s_wal)
            halves(wp[0:H, :, :], w_proj, s_wal)
            row(wp[H:H + 1, 1, :], b_proj, s_wal)
            halves(gv[0:H, :, :], gate_w, s_gw)
            row(gv[H:H + 1, 1, :], gate_b, s_gw)
            for m in range(2):
                sp.dma_start(vw[0:H, m, :], v_w.rearrange("(p a) -> p a", a=1)[H * m:H * m + H]).then_inc(s_gw, 16)
            sp.dma_start(vw[H:H + 1, 1, :], v_b).then_inc(s_gw, 16)
            sp.dma_start(ow[0:E, :], b2).then_inc(s_ow, 16)
            sp.dma_start(ow[E:E + 2, :], out_w).then_inc(s_ow, 16)
            row(ow[E + 2:E + 3, :], out_b, s_ow)
            sp.wait_ge(s_set, filled("bk"))
            sp.dma_start(bk[E:R, :], bk_scale.rearrange("(a n) -> a n", a=1).broadcast_to([3, D])).then_inc(s_ow, 16)

            def load_w1(b):
                w = b % NW
                e = nc.sync.value_load(ebi[0:1, b:b + 1], min_val=0, max_val=E - 1)
                if b >= NW:
                    sp.wait_ge(s_h1, 2 * (b - NW + 1))
                sp.dma_start(W1[0:H, w, :, :], w1[bass.DynSlice(e, 1)].rearrange("e (a p) f -> p (e a) f", p=H)).then_inc(s_w1[w], 16)
                sp.dma_start(W1[H:H + 1, w, 1, :], b1[bass.DynSlice(e, 1)]).then_inc(s_w1[w], 16)

            def load_w2(b):
                w = b % NW
                e = nc.sync.value_load(ebi[0:1, b:b + 1], min_val=0, max_val=E - 1)
                if b >= NW:
                    sp.wait_ge(s_y, b - NW + 1)
                sp.dma_start(W2[:, w, :, :], w2[bass.DynSlice(e, 1)].rearrange("e (m p) n -> p (e m) n", p=P)).then_inc(s_w2[w], 16)

            def load_tokens(b):
                r = nc.sync.value_load(row_i[0:1, b:b + 1], min_val=0, max_val=T * E)
                if b >= 4:
                    sp.wait_ge(s_xg[b % 4], 16 * (b // 4))
                sp.dma_start(xg[:, b, :], xs_dram[bass.DynSlice(r, 1)].rearrange("b p n -> p (b n)")).then_inc(s_xg[b % 4], 16)

            for t in range(T):
                sp.wait_ge(s_dbr, dve_use["proj", t] + 1)
                sp.dma_start(sums[1 + P * t:1 + P * t + ROWS[t], :], h[0:ROWS[t], t, :]).then_inc(s_res, 16)
            sp.wait_ge(s_eb, 1)
            sp.wait_ge(s_w1z, 1)
            load_w1(0)
            sp.wait_ge(s_brow, 1)
            sp.wait_ge(s_sct, 16 * 2 * T)
            load_tokens(0)
            load_tokens(1)
            load_w2(0)
            load_w1(1)
            load_tokens(2)
            load_w2(1)
            load_w1(2)
            for b in range(3, NB):
                load_tokens(b)
                load_w1(b)
                load_w2(b - 1)
                if b == 12:
                    sp.wait_ge(s_side, 16 * len(SIDE))
                    sp.dma_start(acc[:, 0:T - 1, :], side[1:1 + P * (T - 1), :].rearrange("(t p) n -> p t n", p=P)).then_inc(s_sld, 16)
                    sp.dma_start(acc[0:ROWS[T - 1], T - 1, :], side[1 + P * (T - 1):1 + N, :]).then_inc(s_sld, 16)
            load_w2(NB - 1)
            sp.wait_ge(s_add, 16 * (NB - len(SIDE)))
            sp.wait_ge(s_acc, 32)
            sp.dma_start(out.rearrange("b s d -> (b s) d"), sums[1:1 + N, :]).then_inc(s_out, 16)
            sp.wait_ge(s_out, 16)

        @block.gpsimd
        def _(pool):

            def fill(dst, value):
                pool.memset(dst, value).then_inc(s_set, 1)

            pool.dma_start(pc[0:1, :], cls_tok[0]).then_inc(s_pos, 16)
            pool.dma_start(pc[1:S, :], pos_emb).then_inc(s_pos, 16)
            pool.dma_start(bb[1:S, :], tok_b.rearrange("(a n) -> a n", a=1).broadcast_to([NP_, D])).then_inc(s_pos, 16)
            fill(bb[0:1, :], 0.0)
            fill(pT[:, :, :, 0:1], 0.0)
            pool.wait_ge(s_cst, 16)
            pool.tensor_copy(sel[:, :, :], ident[0:S, None, 0:S].broadcast_to([S, B, S])).then_inc(s_sel, 1)
            fill(mv[:, :, :], 1.0)
            fill(eps[:, :], 1e-5)
            fill(half[:, :], -0.5)
            pool.wait_ge(s_pos, 48)
            pool.wait_ge(s_set, filled("bb"))
            pool.tensor_tensor(pc[:, :], pc[:, :], bb[:, :], ALU.add).then_inc(s_pc, 1)
            fill(mT[:, :, :], 1.0)
            fill(xT[:, :, :], 1.0)
            fill(mvz[:, :, :], 0.0)
            fill(q[:, :, N:N + 64], 0.0)
            fill(xrf[:, 2 * XR:2 * XR + P], 0.0)
            fill(Eb[:, :, 4 * M:], 0.0)
            fill(bk[:, :], 1.0)
            fill(one32[:, :], 1.0)
            fill(lg[:, :, :], 0.0)
            fill(m8[:, :, :], 0.0)
            fill(i8[:, :, :], 0)
            fill(ohs[:, :, :], 0.0)
            fill(oneb[:, :], 1.0)
            def rstd_of(t0, t1, n):
                pool.wait_ge(s_ag, t1 if n < len(GROUPS) else T + t1)
                pool.tensor_tensor(rstd[:, t0:t1], mv[:, t0:t1, 1], eps[:, t0:t1], ALU.add).then_inc(s_ve, 1)
                pool.wait_ge(s_ve, n + 1)
                pool.tensor_tensor(rstd[:, t0:t1], rstd[:, t0:t1], half[:, t0:t1], ALU.pow).then_inc(s_rstd, 1)

            for g, (tiles, _) in enumerate(GROUPS):
                rstd_of(tiles[0], tiles[-1] + 1, g)
            pool.wait_ge(s_rstd, len(GROUPS))
            for rows in (aT, a1T, fT, XT):
                fill(rows[H:P], 2.0 if rows is fT else 1.0)
            pool.wait_ge(s_set, filled("XT"))
            fill(feats[:, :], 1.0)
            fill(zero[:, :], 0.0)
            pool.wait_ge(s_set, filled("zero"))
            pool.dma_start(xs_rows.rearrange("(p b) n -> p b n", p=P), zero[:, None, :].broadcast_to([P, T * E + 1, DS])).then_inc(s_zs, 16)
            pool.dma_start(sums[1 + N:, :], zero[:, 0:D]).then_inc(s_dr, 16)
            pool.dma_start(side[1:1 + P * T, :].rearrange("(p t) n -> p t n", t=T), zero[:, None, 0:D].broadcast_to([P, T, D])).then_inc(s_dr, 16)
            pool.dma_start(side[1 + P * T:, :], zero[0:N + P - P * T, 0:D]).then_inc(s_dr, 16)
            pool.tensor_copy(xk[:, :, :, D], const("token")[:, None, :].broadcast_to([P, 2, T])).then_inc(s_id, 1)
            pool.wait_ge(s_id, 1)
            pool.memset(W1[H:P, :, :, :], 0.0).then_inc(s_w1z, 1)
            pool.wait_ge(s_w1z, 1)
            def divide(i):
                m, nh, w = unit_shape(i)
                pool.wait_ge(s_ri, i + 1)
                e = unit_tile(Eb[:, i % NE_, :], i)
                pool.tensor_tensor(e, e, rs[0:m, i % NE_, 0:nh, None].broadcast_to([m, nh, w]), ALU.mult).then_inc(s_pr, 1)

            def scatter(t, k):
                if t == 0:
                    pool.wait_ge(s_zs, 16)
                    pool.wait_ge(s_id, 1)
                pool.wait_ge(s_sl, t + 1)
                pool.wait_ge(s_xk, t + 1)
                pool.indirect_dma_start(out=xs_rows, out_offset=bass.IndirectOffsetOnAxis(ap=sli[0:ROWS[t], t, k:k + 1], axis=0),
                                        in_=xk[0:ROWS[t], k, t, :], in_offset=None).then_inc(s_sct, 16)

            for i in range(STEPS):
                for t in range(T):
                    if i == PROJ[t] + 1:
                        rstd_of(t, t + 1, len(GROUPS) + t)
                if 1 <= i <= NU:
                    divide(i - 1)
                for t in range(T):
                    if i == BLEND[t] + 1 and t < T - 2:
                        blend(pool, t)
                    if i == BLEND[t] and t < T - 2:
                        half_blend(pool, t)
                for t in range(T):
                    for k in range(2):
                        if i == RANK[t] + 1 + k:
                            scatter(t, k)
            pool.wait_ge(s_vrc, 2)
            for r, v in enumerate((vrow, vrev)):
                pool.dma_start(ar[B * r:B * r + B, :], v[:, :].rearrange("p (b s) -> p b s", b=B)).then_inc(s_ar, 16)

            def added(b):
                return len([a for a in range(b) if (a in SIDE) == (b in SIDE)])

            def add_blocks(b0, b1_):
                for b in range(b0, b1_):
                    to, s_to = (side, s_side) if b in SIDE else (sums, s_add)
                    if added(b):
                        pool.wait_ge(s_to, 16 * added(b))
                    pool.wait_ge(s_row, 2 * (b // 4 + 1))
                    pool.wait_ge(s_yc, b + 1)
                    pool.indirect_dma_start(out=to, out_offset=bass.IndirectOffsetOnAxis(ap=slot_row[:, b:b + 1], axis=0),
                                            in_=ysb[:, b % 3, :], in_offset=None, compute_op=ALU.add).then_inc(s_to, 16)

            pool.wait_ge(s_res, 16 * T)
            pool.wait_ge(s_dr, 48)
            add_blocks(0, 9)
            pool.wait_ge(s_sn, 1)
            pool.dma_start(bw[:, :, :], dre[B:2 * B, :, :]).then_inc(s_bwd, 16)
            pool.wait_ge(s_z, 1)
            for r in range(2):
                pool.dma_start(feats[E + r:E + r + 1, :].rearrange("p (b s) -> p b s", b=B), ft[:, r, :]).then_inc(s_fe, 16)
            add_blocks(9, 12)
            pool.wait_ge(s_ba, T)
            pool.wait_ge(s_add, 16 * added(12))
            pool.dma_start(sums[1:1 + P * (T - 1), :].rearrange("(t p) n -> p t n", p=P), acc[:, 0:T - 1, :], accum_op=ALU.add).then_inc(s_acc, 16)
            pool.dma_start(sums[1 + P * (T - 1):1 + N, :], acc[0:ROWS[T - 1], T - 1, :], accum_op=ALU.add).then_inc(s_acc, 16)
            pool.wait_ge(s_acc, 32)
            add_blocks(12, NB)

        @block.scalar
        def _(act):
            for n in range(1, 2 * CK, 2):
                act.wait_ge(s_pt, n + 1)
                c, g = n // 2, n % 2
                act.activation(pT[:, c, :, 1:S].rearrange("p b (gh gw) -> p gw b gh", gw=GRID)[:, 3 * g:3 * g + 3],
                               ps[:, n % 4, 0:3 * B * GRID].rearrange("p (gw b gh) -> p gw b gh", gw=3, b=B),
                               ACT.Copy).then_inc(s_ptc_a, 1)
            act.wait_ge(s_set, filled("xT"))
            for g, (tiles, n) in enumerate(GROUPS):
                act.wait_ge(s_xt, tiles[-1] + 1)
                act.activation(xT[0:H, 1, n], group_bank(g, 1), ACT.Copy).then_inc(s_xtc_a, 1)
            act.wait_ge(s_mt, 1)
            act.wait_ge(s_set, filled("mT"))
            act.activation(mT[0:H, :, :], ps[0:H, 0, 0:256].rearrange("p (a m) -> p a m", a=2)[:, :, 0:M], ACT.Copy).then_inc(s_mtc, 1)
            for a in range(2):
                n = token_half(a)
                act.wait_ge(s_k, 2 * a + 1)
                for j in range(HH):
                    act.activation(kd[:, 0, j, n], ps[:, QK_BANK[a][0], 0:N2], ACT.Copy, scale=headmask[:, j:j + 1]).then_inc(s_kc_a, 1)
                for m in range(2):
                    act.wait_ge(s_q, 2 * a + m + 1)
                    act.activation(q[:, m, n], ps[:, QK_BANK[a][2 + m], 0:N2], ACT.Copy).then_inc(s_qc, 1)
                act.wait_ge(s_xtc_v, a + 1)
                act.activation(*repeated(0, a), ACT.Copy).then_inc(s_xr_a, 1)
                if a == 0:
                    act.wait_ge(s_mkv, 1)
                    for j in range(HH):
                        act.activation(mkd[:, :, j, :], ps[:, 2, 0:256].rearrange("p (a m) -> p a m", a=2)[:, :, 0:M], ACT.Copy,
                                       scale=headmask[:, j:j + 1]).then_inc(s_mkc, 1)

            def exps(i):
                act.wait_ge(s_dbr, dve_use["scores", i] + 1)
                e = unit_tile(Eb[:, i % NE_, :], i)
                act.activation(e, e, ACT.Exp).then_inc(s_exp, 1)

            def copy_probs(i):
                kind, a, g = UNITS[i]
                for r in range(2 if kind == "self" else 1):
                    k = PT0[i] + r
                    u = act_use["probs", i, r]
                    bank = ps[:, ACT_BANK[u % 3], :]
                    act.wait_ge(s_abf, u + 1)
                    if k >= NPT:
                        act.wait_ge(s_o, max(j for j in range(NU) if PT0[j] <= k - NPT) + 1)
                    if kind == "self":
                        act.activation(PTs[:, k % NPT, 0:3 * P], bank[:, 0:3 * P], ACT.Copy).then_inc(s_abr, 1)
                    else:
                        m = ROWS[a]
                        act.activation(PTs[:, k % NPT, :].rearrange("p (c m) -> p c m", c=4)[:, :, 0:m],
                                       bank.rearrange("p (c m) -> p c m", c=4)[:, :, 0:m], ACT.Copy).then_inc(s_abr, 1)

            def halves_bank(u, m):
                return ps[0:H, ACT_BANK[u % 3], 0:2 * P].rearrange("p (a m) -> p a m", a=2)[:, :, 0:m]

            def copy_heads(i):
                kind, a, g = UNITS[i]
                o = ps[0:H, O_BANK, O_COL[kind]:O_COL[kind] + 256].rearrange("p (a m) -> p a m", a=2)
                if kind == "self":
                    w = 2 * S
                    act.wait_ge(s_o, i + 1)
                    act.activation(aT[0:H, :, w * a:w * a + w], o[:, :, 0:w], ACT.Copy).then_inc(s_oc[kind], 1)
                elif g == 2:
                    m = ROWS[a]
                    act.wait_ge(s_o, i + 1)
                    act.activation(a1T[0:H, :, P * a:P * a + m], o[:, :, 0:m], ACT.Copy).then_inc(s_oc[kind], 1)

            def tanh(t):
                u = act_use["blend", t]
                act.wait_ge(s_abf, u + 1)
                if t >= 2:
                    act.wait_ge(s_fu, t - 1)
                act.activation(th[:, t % 2, :, 0:ROWS[t]], halves_bank(u, ROWS[t]), ACT.Tanh, scale=0.5).then_inc(s_abr, 1)

            def copy_tokens(t):
                m = ROWS[t]
                u = act_use["turn", t]
                act.wait_ge(s_abf, u + 1)
                act.activation(xT[0:H, :, P * t:P * t + m], halves_bank(u, m), ACT.Copy).then_inc(s_abr, 1)
                act.activation(xk[0:m, 1, t, 0:D], xk[0:m, 0, t, 0:D], ACT.Copy)

            def gate_exp(t):
                act.wait_ge(s_g1, t + 1)
                act.activation(g2[:, t:t + 1], g1[:, t:t + 1], ACT.Exp).then_inc(s_g2, 1)

            for i in range(STEPS):
                if i < NU:
                    exps(i)
                for j in range(NU):
                    if i == PROBS[j]:
                        copy_probs(j)
                for j in range(NU):
                    if i == HEADS[j]:
                        copy_heads(j)
                for t in range(T):
                    if i == BLEND[t]:
                        tanh(t)
                    if i == TURN[t]:
                        copy_tokens(t)
                    if i == RANK[t]:
                        gate_exp(t)
            for b in range(NB):
                act.wait_ge(s_bt, b + 1)
                act.wait_ge(s_set, filled("XT"))
                act.activation(XT[0:H, b % 2, :, :], ps[0:H, 6 + b % 2, 0:256].rearrange("p (a m) -> p a m", a=2), ACT.Copy).then_inc(s_btc, 1)
                for n in range(2):
                    if n == 0 and b >= 2:
                        act.wait_ge(s_y, b - 1)
                    act.wait_ge(s_h1, 2 * b + n + 1)
                    act.activation(hT[:, b % 2, 3 * n:3 * n + 3, :], ps[:, 2 * (b % 2) + n, 0:3 * P].rearrange("p (f m) -> p f m", f=3),
                                   ACT.Gelu_apprx_tanh).then_inc(s_ge, 1)

        @block.vector
        def _(dve):
            dve.memset(wsb[H:P, :], 0.0).then_inc(s_wz, 1)
            step = {s_sv: 0, s_lgz: 0, s_tk: 0}

            def link(ins, s=s_sv):
                step[s] += 1
                ins.then_inc(s, 1)
                dve.wait_ge(s, step[s])

            for ih in range(IH):
                dve.wait_ge(s_x[ih], 16)
                dve.tensor_copy(xp[:, :, 8 * ih:8 * ih + 8, :], xs[:, 8 * ih:8 * ih + 8, :].rearrange("p i (g j) -> p g i j", g=GW)).then_inc(s_xp, 1)
            dve.wait_ge(s_set, filled("pT"))
            for n in range(0, 2 * CK, 2):
                dve.wait_ge(s_pt, n + 1)
                c, g = n // 2, n % 2
                dve.tensor_copy(pT[:, c, :, 1:S].rearrange("p b (gh gw) -> p gw b gh", gw=GRID)[:, 3 * g:3 * g + 3],
                                ps[:, n % 4, 0:3 * B * GRID].rearrange("p (gw b gh) -> p gw b gh", gw=3, b=B)).then_inc(s_ptc_v, 1)

            def moments(n, t):
                m = ROWS[t]
                dve.bn_stats(st6[0:m, t, :], h[0:m, t, :]).then_inc(s_st, 1)
                dve.wait_ge(s_st, T * n + t + 1)
                dve.bn_aggr(mv[0:m, t, :], st6[0:m, t, :]).then_inc(s_ag, 1)

            def normalise_group(g):
                dve.wait_ge(s_rstd, g + 1)
                for t in GROUPS[g][0]:
                    m = ROWS[t]
                    dve.tensor_scalar(xn[0:m, t, :], h[0:m, t, :], mv[0:m, t, 0:1], rstd[0:m, t:t + 1], ALU.subtract, ALU.mult).then_inc(s_xn, 1)

            dve.wait_ge(s_set, filled("mv"))
            for t in range(T):
                m = ROWS[t]
                dve.wait_ge(s_tok, t + 1)
                dve.tensor_copy(h[0:m, t, :], ps[0:m, 4 + t % 4, 0:D]).then_inc(s_h, 1)
                dve.wait_ge(s_h, t + 1)
                moments(0, t)
                if t == 3:
                    normalise_group(0)

            def copy_group(g):
                tiles, n = GROUPS[g]
                dve.wait_ge(s_xt, tiles[-1] + 1)
                dve.tensor_copy(xT[0:H, 0, n], group_bank(g, 0)).then_inc(s_xtc_v, 1)

            dve.wait_ge(s_set, filled("xT"))
            copy_group(0)
            normalise_group(1)
            copy_group(1)
            for a in range(2):
                n = token_half(a)
                dve.wait_ge(s_xtc_a, a + 1)
                dve.tensor_copy(*repeated(1, a)).then_inc(s_xr_v, 1)
                dve.wait_ge(s_k, 2 * a + 2)
                for j in range(HH):
                    dve.tensor_scalar(kd[:, 1, j, n], ps[:, QK_BANK[a][1], 0:N2], headmask[:, j:j + 1], None, ALU.mult).then_inc(s_kc_v, 1)
                if a == 0:
                    dve.wait_ge(s_mkv, 2)
                    dve.wait_ge(s_set, filled("mvz"))
                    mvv = ps[0:M, 0, 0:D].rearrange("p (j a d) -> p j a d", a=2, d=DH)
                    for a in range(2):
                        dve.tensor_copy(mvz[0:M, a::2, DH * a:DH * a + DH], mvv[:, :, a, :]).then_inc(s_mvc, 1)

            def maxima(i):
                m, nh, w = unit_shape(i)
                u = dve_use["scores", i]
                dve.wait_ge(s_dbf, u + 1)
                dve.tensor_reduce(mx[0:m, i % NE_, 0:nh], unit_tile(ps[:, DVE_BANK[u % 3], :], i), AX_X, ALU.max).then_inc(s_mx, 1)

            def shift(i):
                m, nh, w = unit_shape(i)
                u = dve_use["scores", i]
                if i >= NE_:
                    dve.wait_ge(s_abf, last_probs(i - NE_) + 1)
                dve.wait_ge(s_mx, i + 1)
                dve.tensor_tensor(unit_tile(Eb[:, i % NE_, :], i), unit_tile(ps[:, DVE_BANK[u % 3], :], i),
                                  mx[0:m, i % NE_, 0:nh, None].broadcast_to([m, nh, w]), ALU.subtract).then_inc(s_dbr, 1)

            def sums(i):
                m, nh, w = unit_shape(i)
                dve.wait_ge(s_exp, i + 1)
                dve.tensor_reduce(sm[0:m, i % NE_, 0:nh], unit_tile(Eb[:, i % NE_, :], i), AX_X, ALU.add).then_inc(s_sum, 1)

            def reciprocals(i):
                m, nh, w = unit_shape(i)
                dve.wait_ge(s_sum, i + 1)
                dve.reciprocal(rs[0:m, i % NE_, 0:nh], sm[0:m, i % NE_, 0:nh]).then_inc(s_ri, 1)

            def mask_values(i):
                u = UNITS[i][1]
                dve.wait_ge(s_v, u + 1)
                if u >= 2:
                    dve.wait_ge(s_o, SELF[u - 2] + 1)
                dve.tensor_tensor(vbd[:, u % 2, :, :], ps[:, V_BANK, 0:2 * D].rearrange("p (a n) -> p a n", a=2),
                                  vmask[:, None, :].broadcast_to([P, 2, D]), ALU.mult).then_inc(s_vc, 1)

            def project(t):
                m = ROWS[t]
                u = dve_use["proj", t]
                dve.wait_ge(s_dbf, u + 1)
                dve.scalar_tensor_tensor(out=h[0:m, t, :], in0=ps[0:m, DVE_BANK[u % 3], 0:D], scalar=0.5, in1=h[0:m, t, :],
                                         op0=ALU.mult, op1=ALU.add).then_inc(s_dbr, 1)
                dve.wait_ge(s_dbr, u + 1)
                moments(1, t)

            def normalise(t):
                m = ROWS[t]
                dve.wait_ge(s_rstd, len(GROUPS) + t + 1)
                dve.tensor_scalar(xk[0:m, 0, t, 0:D], h[0:m, t, :], mv[0:m, t, 0:1], rstd[0:m, t:t + 1], ALU.subtract, ALU.mult).then_inc(s_xn, 1)

            def choose(t):
                m = ROWS[t]
                u = dve_use["gate", t]
                dve.wait_ge(s_dbf, u + 1)
                dve.tensor_copy(lg[0:m, t, :], ps[0:m, DVE_BANK[u % 3], 0:E]).then_inc(s_dbr, 1)
                dve.wait_ge(s_dbr, u + 1)
                link(dve.max(m8[:, t, :], lg[:, t, :]), s_tk)
                link(dve.max_index(i8[:, t, :], m8[:, t, :], lg[:, t, :]), s_tk)
                dve.tensor_tensor(g1[:, t:t + 1], m8[:, t, 1:2], m8[:, t, 0:1], ALU.subtract).then_inc(s_g1, 1)
                link(dve.tensor_tensor(i8f[:, :], i8[:, t, 0:2], const("no_token")[:, t:t + 1].broadcast_to([P, 2]), ALU.add), s_tk)
                link(dve.tensor_tensor(oh[:, :, t, :], i8f[:, :, None].broadcast_to([P, 2, E]), const("iota")[:, None, :].broadcast_to([P, 2, E]),
                                       ALU.is_equal), s_tk)
                dve.tensor_tensor(ohs[:, t, :], oh[:, 0, t, :], oh[:, 1, t, :], ALU.add).then_inc(s_oh, 1)

            def place(t):
                u = dve_use["rank", t]
                rank = ps[:, DVE_BANK[u % 3], 0:2 * E]
                dve.wait_ge(s_dbf, u + 1)
                ins = dve.tensor_tensor(rb[:, :], rank[:, 0:E], const("region"), ALU.add)
                if t == T - 1:
                    link(ins, s_lgz)
                else:
                    ins.then_inc(s_dbr, 1)
                    dve.wait_ge(s_dbr, u + 1)
                link(dve.tensor_tensor(sl3[:, :, :], oh[:, :, t, :], rb[:, None, :].broadcast_to([P, 2, E]), ALU.mult), s_lgz)
                link(dve.tensor_reduce(slf[:, :], sl3[:, :, :], AX_X, ALU.add), s_lgz)
                dve.tensor_copy(sli[:, t, :], slf[:, :]).then_inc(s_sl, 1)
                dve.wait_ge(s_g2, t + 1)
                link(dve.tensor_scalar(g3[:, t:t + 1], g2[:, t:t + 1], 1.0, None, ALU.add), s_lgz)
                link(dve.reciprocal(xk[:, 0, t, D + 1:D + 2], g3[:, t:t + 1]), s_lgz)
                dve.tensor_tensor(xk[:, 1, t, D + 1:D + 2], g2[:, t:t + 1], xk[:, 0, t, D + 1:D + 2], ALU.mult).then_inc(s_xk, 1)

            dve.tensor_copy(trib[:, :], const("before"))
            dve.wait_ge(s_set, len(FILLS))
            for i in range(STEPS):
                if i < NU:
                    maxima(i)
                if 1 <= i <= NU:
                    sums(i - 1)
                if i < NU:
                    shift(i)
                if 1 <= i <= NU:
                    reciprocals(i - 1)
                if i < NU and UNITS[i][0] == "self":
                    mask_values(i)
                for t in range(T):
                    if i == BLEND[t] and t >= T - 2:
                        half_blend(dve, t)
                        blend(dve, t)
                    if i == PROJ[t]:
                        project(t)
                    if i == PROJ[t] + 1:
                        normalise(t)
                    if i == GATE[t]:
                        choose(t)
                    if i == RANK[t]:
                        place(t)

            def route(ins):
                link(ins, s_lgz)

            total = ps[:, DVE_BANK[dve_use["rank", T - 1] % 3], E:2 * E]
            route(dve.tensor_tensor(cmp5[:, :, :], total[:, :, None].broadcast_to([P, E, T]), const("blocks_from")[:, None, :].broadcast_to([P, E, T]), ALU.is_gt))
            route(dve.tensor_reduce(nblk[:, :], cmp5[:, :, :], AX_X, ALU.add))
            dve.tensor_scalar(gap[:, :], nblk[0:1, :], -1.0, float(T), ALU.mult, ALU.add)
            route(dve.tensor_tensor(cmp8[:, :, :], nblk[:, None, :].broadcast_to([P, E, E]), const("through").rearrange("p (a e) -> p a e", a=E), ALU.mult))
            route(dve.tensor_reduce(cend[:, :], cmp8[:, :, :], AX_X, ALU.add))
            route(dve.tensor_tensor(cmpb[:, :, :], const("block", 1)[:, :, None].broadcast_to([1, NB, E]), cend[0:1, None, :].broadcast_to([1, NB, E]), ALU.is_ge))
            route(dve.tensor_reduce(ebf[:, :], cmpb[:, :, :], AX_X, ALU.add))
            dve.tensor_scalar(ebi[:, :], ebf[:, :], float(E - 1), None, ALU.min).then_inc(s_eb, 1)
            route(dve.tensor_tensor(gapb[:, :, :], cmpb[:, :, :], gap[:, None, :].broadcast_to([1, NB, E]), ALU.mult))
            route(dve.tensor_reduce(row_f[:, :], gapb[:, :, :], AX_X, ALU.add))
            route(dve.tensor_tensor(row_f[:, :], row_f[:, :], const("block", 1), ALU.add))
            dve.tensor_scalar(row_i[:, :], row_f[:, :], float(T * E), None, ALU.min).then_inc(s_brow, 1)
            dve.wait_ge(s_vr, 1)
            dve.tensor_scalar(vrow[:, :].rearrange("p (a n) -> p a n", a=2), ps[0:1, 4:6, 0:N2], -3.0, 3.0, ALU.max, ALU.min).then_inc(s_vrc, 1)
            dve.wait_ge(s_vrc, 1)
            dve.tensor_copy(vrev[:, :].rearrange("p (b s) -> p b s", b=B), vrow[:, :].rearrange("p (b s) -> p b s", b=B)[:, :, ::-1]).then_inc(s_vrc, 1)
            for k in range(2):
                route(dve.tensor_tensor(comb[:, k, :, :], oh[:, k, :, :], xk[:, k, :, D + 1:D + 2].broadcast_to([P, T, E]), ALU.mult))
            dve.tensor_tensor(comb[:, 0, :, :], comb[:, 0, :, :], comb[:, 1, :, :], ALU.add).then_inc(s_cb, 1)

            def copy_block(b):
                if b % 4 == 0:
                    n = slice(b, min(b + 4, NB))
                    for r in range(b, min(b + 4, NB)):
                        dve.wait_ge(s_xg[r % 4], 16 * (r // 4 + 1))
                    dve.tensor_scalar(slot_dummy[:, n], xg[:, n, D], 0.0, const("dummy"), ALU.is_equal, ALU.mult).then_inc(s_row, 1)
                    dve.wait_ge(s_row, b // 2 + 1)
                    dve.tensor_tensor(slot_row[:, n], xg[:, n, D], slot_dummy[:, n], ALU.add).then_inc(s_row, 1)
                dve.wait_ge(s_y, b + 1)
                if b >= 3:
                    a = b - 3
                    dve.wait_ge(s_side if a in SIDE else s_add, 16 * len([c for c in range(a + 1) if (c in SIDE) == (a in SIDE)]))
                dve.tensor_scalar(ysb[:, b % 3, :], ps[:, 4 + b % 2, 0:D], xg[:, b, D + 1:D + 2], None, ALU.mult).then_inc(s_yc, 1)

            dve.wait_ge(s_ct, 1)
            dve.wait_ge(s_set, filled("feats"))
            dve.tensor_copy(feats[0:E, :], psf[0:E, 4 * 512:4 * 512 + N]).then_inc(s_ctc, 1)
            dve.wait_ge(s_ar, 32)
            link(dve.tensor_scalar(ar[:, :], ar[:, :], -2.0, None, ALU.add))
            link(dve.tensor_tensor(asg[:, :], ar[:, :], const("alternate", 2 * B), ALU.mult))
            dve.tensor_copy(dre[:, 0, 1:2], one32[:, :])
            link(dve.tensor_copy(dre[:, 0, 0:1], asg[:, 0:1]))
            for n in range(1, S):
                if n % 4 == 3:
                    copy_block(n // 4)
                link(dve.tensor_tensor(dsq[:, :], dre[:, n - 1, :], dre[:, n - 1, :], ALU.mult))
                link(dve.tensor_reduce(dn[:, :], dsq[:, :], AX_X, ALU.add))
                link(dve.reciprocal(dri[:, :], dn[:, :]))
                dve.tensor_scalar(dre[:, n, 0:1], dre[:, n - 1, 0:1], dri[:, 0:1], asg[:, n:n + 1], ALU.mult, ALU.add)
                link(dve.tensor_scalar(dre[:, n, 1:2], dre[:, n - 1, 1:2], dri[:, 0:1], 1.0, ALU.mult, ALU.add))
            dve.tensor_tensor(dre[:, :, 0], dre[:, :, 0], const("alternate", 2 * B), ALU.mult).then_inc(s_sn, 1)
            dve.wait_ge(s_bwd, 16)
            rev = bw[:, ::-1, :]
            link(dve.tensor_tensor(z[:, :, :], dre[0:B, :, :], rev, ALU.add))
            link(dve.tensor_tensor(z[:, :, 0], z[:, :, 0], ar[0:B, :], ALU.subtract))
            link(dve.tensor_scalar(z[:, :, 1], z[:, :, 1], -1.0, None, ALU.add))
            link(dve.tensor_tensor(zz[:, :, :], z[:, :, :], z[:, :, :], ALU.mult))
            link(dve.tensor_reduce(zn[:, :], zz[:, :, :], AX_X, ALU.add))
            link(dve.reciprocal(zr[:, :], zn[:, :]))
            link(dve.tensor_tensor(ft[:, :, :], z[:, :, :].rearrange("p s c -> p c s"), zr[:, None, :].broadcast_to([B, 2, S]), ALU.mult))
            dve.tensor_scalar(ft[:, :, :], ft[:, :, :], -10.0, 10.0, ALU.max, ALU.min).then_inc(s_z, 1)
            dve.wait_ge(s_ow, 64)
            dve.tensor_tensor(ow[:, :], ow[:, :], bk[:, :], ALU.mult).then_inc(s_owb, 1)
            for b in range(9, NB):
                if b == 12:
                    for t in range(T):
                        m = ROWS[t]
                        dve.wait_ge(s_sp, t + 1)
                        dve.wait_ge(s_sld, 32)
                        dve.tensor_tensor(acc[0:m, t, :], ps[0:m, 6 + t % 2, 256:256 + D], acc[0:m, t, :], ALU.add).then_inc(s_ba, 1)
                copy_block(b)

        @block.tensor
        def _(pe):
            pe.wait_ge(s_cst, 16)
            for _ in range(4):
                pe.matmul(ps[:, 7, 0:3 * P], ident, cst[:, 0:3 * P], start=True, stop=True)
            for n in range(2 * CK):
                c, g = n // 2, n % 2
                if n >= 4:
                    if n % 2:
                        pe.wait_ge(s_ptc_a, (n - 4) // 2 + 1)
                    else:
                        pe.wait_ge(s_ptc_v, (n - 4) // 2 + 1)
                pe.wait_ge(s_xp, c // (CK // IH) + 1)
                for a in range(3):
                    patch = xp[:, 3 * g + a, :, :].rearrange("p i j -> p (i j)")
                    ins = pe.transpose(ps[:, n % 4, a * 96:a * 96 + 96], patch[:, P * c:P * c + P], ident[0:96, 0:96])
                ins.then_inc(s_pt, 1)
            pe.wait_ge(s_sel, 1)
            pe.wait_ge(s_pc, 1)
            pe.wait_ge(s_wt, 16)
            pe.wait_ge(s_ptc_a, CK)
            pe.wait_ge(s_ptc_v, CK)
            self_ = sel[:, :, :].rearrange("p b s -> p (b s)")
            for t in range(T):
                m = ROWS[t]
                if t >= 4:
                    pe.wait_ge(s_h, t - 3)
                o = ps[0:m, 4 + t % 4, 0:D]
                pe.matmul(o, self_[:, P * t:P * t + m], pc[:, :], start=True, stop=False)
                for c in range(CK):
                    ins = pe.matmul(o, pT[:, c, :, :].rearrange("p b s -> p (b s)")[:, P * t:P * t + m], wt[:, c, :],
                                    start=False, stop=(c == CK - 1))
                ins.then_inc(s_tok, 1)
            def memory_products():
                pe.wait_ge(s_mtc, 1)
                pe.wait_ge(s_xtc_a, 1)
                for m in range(2):
                    o = ps[:, 2, 128 * m:128 * m + M]
                    pe.matmul(o, wm[:, 0, H * m:H * m + P], mT[:, 0, :], start=True, stop=False)
                    ins = pe.matmul(o, wm[:, 1, H * m:H * m + P], mT[:, 1, :], start=False, stop=True)
                ins.then_inc(s_mkv, 1)
                pe.matmul(ps[0:M, 0, 0:D], mT[:, 0, :], wm[:, 0, D:2 * D], start=True, stop=False)
                pe.matmul(ps[0:M, 0, 0:D], mT[:, 1, :], wm[:, 1, D:2 * D], start=False, stop=True).then_inc(s_mkv, 1)

            for g, (tiles, _) in enumerate(GROUPS):
                for t in tiles:
                    m = ROWS[t]
                    c = P * (t - tiles[0])
                    pe.wait_ge(s_xn, t + 1)
                    for a in range(2):
                        ins = pe.transpose(group_bank(g, a)[:, c:c + m], xn[0:m, t, H * a:H * a + H], ident[0:m, 0:m])
                    ins.then_inc(s_xt, 1)
            pe.wait_ge(s_mem, 48)
            pe.wait_ge(s_xtc_v, 1)
            for m in range(2):
                ins = pe.transpose(ps[0:H, 0, 128 * m:128 * m + M], mf[:, H * m:H * m + H], ident[0:M, 0:M])
            ins.then_inc(s_mt, 1)
            pe.wait_ge(s_wat, 32)
            pe.wait_ge(s_h, T)
            for a in range(2):
                if a == 1:
                    memory_products()
                pe.wait_ge(s_xtc_a, a + 1)
                pe.wait_ge(s_xtc_v, a + 1)
                for b, col in enumerate((D, D + H, 0, H)):
                    if (a, b) == (1, 2):
                        pe.wait_ge(s_mvc, 2)
                        pe.wait_ge(s_mkc, HH)
                    o = ps[:, QK_BANK[a][b], 0:N2]
                    pe.matmul(o, wa[:, 0, col:col + P], xT[:, 0, token_half(a)], start=True, stop=False)
                    pe.matmul(o, wa[:, 1, col:col + P], xT[:, 1, token_half(a)], start=False, stop=True).then_inc(s_k if b < 2 else s_q, 1)
            pe.wait_ge(s_qc, 4)
            pe.wait_ge(s_kc_a, 2 * HH)
            pe.wait_ge(s_kc_v, 2 * HH)
            pe.wait_ge(s_xr_a, 2)
            pe.wait_ge(s_xr_v, 2)

            def dve_bank(u):
                if u >= 3:
                    pe.wait_ge(s_dbr, u - 2)
                return ps[:, DVE_BANK[u % 3], :]

            def act_bank(u):
                if u >= 3:
                    pe.wait_ge(s_abr, u - 2)
                return ps[:, ACT_BANK[u % 3], :]

            def scores(i):
                kind, a, g = UNITS[i]
                s = dve_bank(dve_use["scores", i])
                if kind == "self":
                    for r in range(2):
                        n0 = (2 * a + r) * S
                        for m in range(2):
                            ins = pe.matmul(s[64 * r:64 * r + 64, HH * S * m:HH * S * (m + 1)], q[:, m, n0:n0 + 64],
                                            kd[:, m, :, n0:n0 + S], start=True, stop=True)
                else:
                    rows = ROWS[a]
                    for m, h0, h1, c0_ in (((0, 0, 4, 0),), ((0, 4, 6, 0), (1, 0, 2, 2 * M)), ((1, 2, 6, 0),))[g]:
                        ins = pe.matmul(s[0:rows, c0_:c0_ + (h1 - h0) * M], q[:, m, P * a:P * a + rows], mkd[:, m, h0:h1, :],
                                        start=True, stop=True)
                ins.then_inc(s_dbf, 1)

            def values(i):
                u = UNITS[i][1]
                if u >= 1:
                    pe.wait_ge(s_vc, u)
                for r in range(2):
                    o = ps[:, V_BANK, D * r:D * (r + 1)]
                    c = (2 * u + r) * 2 * S
                    pe.matmul(o, xrf[:, c:c + P], wa[:, 0, 2 * D:3 * D], start=True, stop=False)
                    ins = pe.matmul(o, xrf[:, XR + c:XR + c + P], wa[:, 1, 2 * D:3 * D], start=False, stop=True)
                ins.then_inc(s_v, 1)

            def transposes(i):
                kind, a, g = UNITS[i]
                e = Eb[:, i % NE_, :]
                pe.wait_ge(s_pr, i + 1)
                for r in range(2 if kind == "self" else 1):
                    o = act_bank(act_use["probs", i, r])
                    if kind == "self":
                        for c in range(3):
                            h0 = 2 * (3 * r + c) * S
                            ins = pe.transpose(o[:, P * c:P * c + P], e[:, h0:h0 + P], ident)
                    else:
                        m = ROWS[a]
                        for c in range(4):
                            ins = pe.transpose(o[:, P * c:P * c + m], e[0:m, c * M:c * M + P], ident[0:m, 0:m])
                    ins.then_inc(s_abf, 1)

            def heads(i):
                kind, a, g = UNITS[i]
                o = ps[:, O_BANK, O_COL[kind]:O_COL[kind] + 256]
                for before in ("self", "mem"):
                    n = len([j for j in range(i) if UNITS[j][0] == before and (before == "self" or UNITS[j][2] == 2)])
                    if n:
                        pe.wait_ge(s_oc[before], n)
                if kind == "self":
                    pe.wait_ge(s_abr, last_probs(i) + 1)
                    pe.wait_ge(s_vc, a + 1)
                    for c in range(6):
                        pt = PTs[:, (PT0[i] + c // 3) % NPT, P * (c % 3):P * (c % 3) + P]
                        for r in range(2):
                            c0_ = (c // 3) * P + r * S
                            ins = pe.matmul(o[32 * (c % 3):32 * (c % 3) + 32, c0_:c0_ + S], vbd[:, a % 2, r, 32 * c:32 * c + 32],
                                            pt[:, 64 * r:64 * r + S], start=True, stop=True)
                else:
                    pe.wait_ge(s_abr, last_probs(i) + 1)
                    m = ROWS[a]
                    pt = PTs[:, PT0[i] % NPT, :]
                    for c in range(4):
                        j = 2 * g + c // 2
                        ins = pe.matmul(o[32 * (j % 3):32 * (j % 3) + 32, (j // 3) * P:(j // 3) * P + m], mvz[:, 4 * g + c, :],
                                        pt[:, P * c:P * c + m], start=(c % 2 == 0), stop=(c % 2 == 1))
                ins.then_inc(s_o, 1)

            def blend(t):
                m = ROWS[t]
                n = slice(P * t, P * t + m)
                o = act_bank(act_use["blend", t])
                pe.wait_ge(s_wal, 64)
                pe.wait_ge(s_oc["self"], PAIRS[t])
                pe.wait_ge(s_oc["mem"], t + 1)
                for a in range(2):
                    c = slice(H * a, H * a + H)
                    z = o[0:H, P * a:P * a + m]
                    for k, (w, x_) in enumerate(((0, aT[:, 0, n]), (1, aT[:, 1, n]), (2, a1T[:, 0, n]), (3, a1T[:, 1, n]))):
                        ins = pe.matmul(z, wal[:, w, c], x_, start=(k == 0), stop=(k == 3))
                ins.then_inc(s_abf, 1)

            def project_tile(t):
                m = ROWS[t]
                n = slice(P * t, P * t + m)
                o = dve_bank(dve_use["proj", t])[0:m, 0:D]
                pe.wait_ge(s_ft, t + 1)
                pe.matmul(o, fT[:, 0, n], wp[:, 0, :], start=True, stop=False)
                pe.matmul(o, fT[:, 1, n], wp[:, 1, :], start=False, stop=True).then_inc(s_dbf, 1)

            def turn(t):
                m = ROWS[t]
                o = act_bank(act_use["turn", t])
                pe.wait_ge(s_xn, T + t + 1)
                pe.transpose(o[0:H, 0:m], xk[0:m, 0, t, 0:H], ident[0:m, 0:m])
                pe.transpose(o[0:H, P:P + m], xk[0:m, 0, t, H:D], ident[0:m, 0:m]).then_inc(s_abf, 1)

            def gate(t):
                m = ROWS[t]
                n = slice(P * t, P * t + m)
                o = dve_bank(dve_use["gate", t])[0:m, 0:E]
                pe.wait_ge(s_gw, 80)
                pe.wait_ge(s_abr, act_use["turn", t] + 1)
                pe.matmul(o, xT[:, 0, n], gv[:, 0, :], start=True, stop=False)
                pe.matmul(o, xT[:, 1, n], gv[:, 1, :], start=False, stop=True).then_inc(s_dbf, 1)

            def rank(t):
                o = dve_bank(dve_use["rank", t])
                pe.wait_ge(s_oh, t + 1)
                ins = pe.matmul(o[:, 0:E], trib[:, :], ohs[:, t, :], start=True, stop=(t == 0))
                for r in range(t):
                    ins = pe.matmul(o[:, 0:E], oneb[:, :], ohs[:, r, :], start=False, stop=(r == t - 1))
                if t == T - 1:
                    for r in range(T):
                        ins = pe.matmul(o[:, E:2 * E], oneb[:, :], ohs[:, r, :], start=(r == 0), stop=(r == T - 1))
                ins.then_inc(s_dbf, 1)

            for i in range(STEPS):
                if i < NU:
                    scores(i)
                    if UNITS[i][0] == "self":
                        values(i)
                for j in range(NU):
                    if i == PROBS[j]:
                        transposes(j)
                for j in range(NU):
                    if i == HEADS[j]:
                        heads(j)
                for t in range(T):
                    if i == BLEND[t]:
                        blend(t)
                    if i == PROJ[t]:
                        project_tile(t)
                    if i == TURN[t]:
                        turn(t)
                    if i == GATE[t]:
                        gate(t)
                    if i == RANK[t]:
                        rank(t)
            for a in range(2):
                n = slice(a * N2, (a + 1) * N2)
                pe.matmul(ps[0:1, 4 + a, 0:N2], vw[:, 0, :], xT[:, 0, n], start=True, stop=False)
                ins = pe.matmul(ps[0:1, 4 + a, 0:N2], vw[:, 1, :], xT[:, 1, n], start=False, stop=True)
            ins.then_inc(s_vr, 1)
            pe.wait_ge(s_abr, len(act_use))
            for _ in range(4):
                pe.matmul(ps[:, 2, 0:3 * P], ident, cst[:, 0:3 * P], start=True, stop=True)

            def turn_shares():
                pe.wait_ge(s_cb, 1)
                pe.wait_ge(s_vrc, 1)
                for t in range(T):
                    m = ROWS[t]
                    ins = pe.transpose(psf[0:E, 4 * 512 + P * t:4 * 512 + P * t + m], comb[0:m, 0, t, :], ident[0:m, 0:m])
                ins.then_inc(s_ct, 1)

            def spread(b):
                pe.wait_ge(s_xg[b % 4], 16 * (b // 4 + 1))
                if b >= 2:
                    pe.wait_ge(s_btc, b - 1)
                for m in range(2):
                    ins = pe.transpose(ps[0:H, 6 + b % 2, P * m:P * m + P], xg[:, b, H * m:H * m + H], ident)
                ins.then_inc(s_bt, 1)

            def hidden(b):
                w = b % NW
                pe.wait_ge(s_w1[w], 32 * (b // NW + 1))
                pe.wait_ge(s_btc, b + 1)
                if b >= 2:
                    pe.wait_ge(s_ge, 2 * b - 2)
                for f in range(FM):
                    o = ps[:, 2 * (b % 2) + f // 3, P * (f % 3):P * (f % 3) + P]
                    pe.matmul(o, W1[:, w, 0, P * f:P * f + P], XT[:, b % 2, 0, :], start=True, stop=False)
                    ins = pe.matmul(o, W1[:, w, 1, P * f:P * f + P], XT[:, b % 2, 1, :], start=False, stop=True)
                    if f % 3 == 2:
                        ins.then_inc(s_h1, 1)

            def outputs(b):
                w = b % NW
                if b >= 2:
                    pe.wait_ge(s_yc, b - 1)
                pe.wait_ge(s_w2[w], 16 * (b // NW + 1))
                o = ps[:, 4 + b % 2, 0:D]
                for f in range(FM):
                    if f % 3 == 0:
                        pe.wait_ge(s_ge, 2 * b + f // 3 + 1)
                    ins = pe.matmul(o, hT[:, b % 2, f, :], W2[:, w, f, :], start=(f == 0), stop=(f == FM - 1))
                ins.then_inc(s_y, 1)

            spread(0)
            for b in range(NB):
                if b + 1 < NB:
                    spread(b + 1)
                hidden(b)
                if b == 0:
                    turn_shares()
                if b == 1:
                    pe.wait_ge(s_ctc, 1)
                if b >= 1:
                    outputs(b - 1)
                if b == 12:
                    pe.wait_ge(s_owb, 1)
                    pe.wait_ge(s_fe, 32)
                    for t in range(T):
                        m = ROWS[t]
                        if t >= 2:
                            pe.wait_ge(s_ba, t - 1)
                        pe.wait_ge(s_btc, 14)
                        pe.matmul(ps[0:m, 6 + t % 2, 256:256 + D], feats[:, P * t:P * t + m], ow[:, :], start=True, stop=True).then_inc(s_sp, 1)
                    pe.wait_ge(s_ba, T)
            outputs(NB - 1)


_INS = ["x", "cls_tok", "L0_tok_W", "L0_tok_b", "L0_tok_pos_emb", "L0_attn_w_attn", "L0_attn_b_attn", "L0_attn_w_proj",
        "L0_attn_b_proj", "L0_attn_w_mem", "L0_attn_b_mem", "L0_attn_w_alpha", "L0_attn_b_alpha", "L0_attn_memory_features",
        "L0_ffn_v_w", "L0_ffn_v_b", "L0_ffn_gate_w", "L0_ffn_gate_b", "L0_ffn_w1", "L0_ffn_b1", "L0_ffn_w2", "L0_ffn_b2",
        "L0_ffn_out_w", "L0_ffn_out_b", "L0_ffn_bk_scale"]


def kernel(**inputs):
    import numpy as _np
    import concourse.bacc as _bacc
    from concourse import mybir as _mybir
    from concourse.bass_utils import run_bass_kernel_spmd as _run

    nc = _bacc.Bacc("TRN2", target_bir_lowering=False, num_devices=1)
    arrays, args = {}, []
    for name in _INS:
        a = _np.ascontiguousarray(inputs[name])
        if a.ndim == 0:
            a = a.reshape(1, 1)
        arrays[f"in_{name}"] = a
        args.append(nc.dram_tensor(f"in_{name}", a.shape, _mybir.dt.from_np(a.dtype), kind="ExternalInput").ap())
    p = _np.arange(128)[:, None]
    e = _np.arange(8)
    tables = {
        "ident": p == _np.arange(128),
        "headmask": p // 16 == _np.arange(6),
        "vmask": p // 37 == (_np.arange(192) // 16) % 2,
        "iota": e + 0 * p,
        "blocks_from": 128 * _np.arange(5) + 0 * p,
        "through": (e[None, :] <= e[:, None]).reshape(1, 64) + 0 * p,
        "block": _np.arange(17) + 0 * p,
        "no_token": 100 * (128 * _np.arange(5) + p >= 592),
        "before": p < _np.arange(128),
        "region": 640 * e + 0 * p,
        "token": 128 * _np.arange(5) + p + 1,
        "dummy": 593 + p,
        "alternate": 1 - 2 * (_np.arange(37) % 2) + 0 * p,
    }
    consts = _np.concatenate([tables[name] for name, _ in CONSTS], axis=1).astype(_np.float32)
    arrays["in_consts"] = consts
    args.append(nc.dram_tensor("in_consts", consts.shape, _mybir.dt.float32, kind="ExternalInput").ap())
    args.append(nc.dram_tensor("out_0", (16, 37, 192), _mybir.dt.float32, kind="ExternalOutput").ap())
    vit_block(nc, *args)
    r = _run(nc, [arrays], core_ids=[0])
    return r.results[0]["out_0"]
```
